# Optimizing a Trainium2 kernel written in Bass

```python
import numpy as np
import jax
import jax.numpy as jnp

def _softmax(x, axis=-1):
    return jax.nn.softmax(x, axis=axis)

def _gelu(x):
    return jax.nn.gelu(x, approximate=True)

def _silu(x):
    return jax.nn.silu(x)

def _sigmoid(x):
    return jax.nn.sigmoid(x)

def _layernorm(x, axis=-1, eps=1e-05):
    m = jnp.mean(x, axis=axis, keepdims=True)
    v = jnp.var(x, axis=axis, keepdims=True)
    return (x - m) / jnp.sqrt(v + eps)

def _scatter_add(tgt, idx, src, axis=0):
    return tgt.at[idx].add(src)

def _segment_sum(src, seg, n):
    return jax.ops.segment_sum(src, seg, n)
kernel_name = 'mk_gnn_resnorm_d4_gnn_r16_474067'

def setup_inputs(seed: int=0):
    np.random.seed(seed)
    _w = jnp.asarray

    def _rec_inputs():
        import jax
        import jax.numpy as jnp
        _gk = jax.random.key(seed)
        x = -6.415e-05 + 1 * jax.random.normal(jax.random.fold_in(_gk, 1), (1250, 512), jnp.float32)
        src = jax.random.randint(jax.random.fold_in(_gk, 2), (40000,), 0, 1250, jnp.int32)
        dst = jax.random.randint(jax.random.fold_in(_gk, 3), (40000,), 0, 1250, jnp.int32)
        _o = jnp.argsort(dst, stable=True)
        src = src[_o]
        dst = dst[_o]
        edge_attr_20 = jax.random.uniform(jax.random.fold_in(_gk, 12), (40000, 20), jnp.float32, 0.0, 0.999999)
        edge_attr_3 = -0.0005747 + 0.998114 * jax.random.normal(jax.random.fold_in(_gk, 13), (40000, 3), jnp.float32)
        edge_weight = jax.random.uniform(jax.random.fold_in(_gk, 15), (40000,), jnp.float32, 0.0, 0.999999)
        return (x, src, dst, edge_attr_20, edge_attr_3, edge_weight)
    x, src, dst, edge_attr_20, edge_attr_3, edge_weight = _rec_inputs()

    def _L0_gnn_setup():
        import jax, jax.numpy as jnp
        import numpy as np
        N_NODES = 1250
        key = jax.random.key(seed)
        ks = jax.random.split(key, 6)
        d = 512
        E = 40000
        x = jax.random.normal(ks[0], (N_NODES, d), dtype=jnp.float32)
        edge_index = jax.random.randint(ks[1], (2, E), 0, N_NODES, dtype=jnp.int64)
        s = 1.0 / np.sqrt(d)
        W1 = jax.random.uniform(ks[2], (d, d), jnp.float32, -s, s)
        b1 = jax.random.uniform(ks[3], (d,), jnp.float32, -s, s)
        W2 = jax.random.uniform(ks[4], (d, d), jnp.float32, -s, s)
        b2 = jax.random.uniform(ks[5], (d,), jnp.float32, -s, s)
        return {'x': x, 'edge_index': edge_index, 'W1': W1, 'b1': b1, 'W2': W2, 'b2': b2}
    _L0_gnn_all = _L0_gnn_setup()
    _L0_gnn_in = {k: v for k, v in _L0_gnn_all.items() if k in ('W1', 'b1', 'W2', 'b2')}
    del _L0_gnn_all

    def _L1_gnn_setup():
        import jax, jax.numpy as jnp
        import numpy as np
        N, E, D = (625, 10000, 512)

        def _sage_layer(h, src, dst, W_self, W_neigh, b, n_nodes):
            agg = jax.ops.segment_sum(h[src], dst, num_segments=n_nodes)
            deg = jax.ops.segment_sum(jnp.ones_like(dst, dtype=h.dtype), dst, num_segments=n_nodes)
            h_neigh = agg / jnp.maximum(deg, 1.0)[:, None]
            return jax.nn.relu(h @ W_self + h_neigh @ W_neigh + b)
        key = jax.random.key(seed)
        ks = jax.random.split(key, 8)
        scale = 1.0 / np.sqrt(D)
        return {'feats': jax.random.normal(ks[0], (N, D), dtype=jnp.float32), 'src': jax.random.randint(ks[1], (E,), 0, N, dtype=jnp.int32), 'dst': jax.random.randint(ks[2], (E,), 0, N, dtype=jnp.int32), 'W_self1': jax.random.normal(ks[3], (D, D), dtype=jnp.float32) * scale, 'W_neigh1': jax.random.normal(ks[4], (D, D), dtype=jnp.float32) * scale, 'b1': jnp.zeros((D,), dtype=jnp.float32), 'W_self2': jax.random.normal(ks[5], (D, D), dtype=jnp.float32) * scale, 'W_neigh2': jax.random.normal(ks[6], (D, D), dtype=jnp.float32) * scale, 'b2': jnp.zeros((D,), dtype=jnp.float32)}
    _L1_gnn_all = _L1_gnn_setup()
    _L1_gnn_in = {k: v for k, v in _L1_gnn_all.items() if k in ('W_self1', 'W_neigh1', 'b1', 'W_self2', 'W_neigh2', 'b2')}
    del _L1_gnn_all

    def _L2_gnn_setup():
        import jax, jax.numpy as jnp
        import numpy as np
        N_NODES = 3125
        N_EDGES = 100000
        D_FEAT = 512
        UNITS = 512
        key = jax.random.key(seed)
        k1, k2, k3, k4, k5 = jax.random.split(key, 5)
        X = jax.random.normal(k1, (N_NODES, D_FEAT), dtype=jnp.float32)
        W = jax.random.normal(k2, (D_FEAT, UNITS), dtype=jnp.float32) * (1.0 / np.sqrt(D_FEAT))
        bias = jnp.zeros((UNITS,), dtype=jnp.float32)
        edge_weight = jax.random.uniform(k3, (N_EDGES,), dtype=jnp.float32)
        edge_src = jax.random.randint(k4, (N_EDGES,), 0, N_NODES, dtype=jnp.int64)
        edge_dst = jax.random.randint(k5, (N_EDGES,), 0, N_NODES, dtype=jnp.int64)
        return {'X': X, 'W': W, 'bias': bias, 'edge_weight': edge_weight, 'edge_src': edge_src, 'edge_dst': edge_dst}
    _L2_gnn_all = _L2_gnn_setup()
    _L2_gnn_in = {k: v for k, v in _L2_gnn_all.items() if k in ('W', 'bias')}
    del _L2_gnn_all

    def _L3_gnn_setup():
        import jax, jax.numpy as jnp
        import numpy as np
        N_ATOMS = 5000
        N_EDGES = 3125
        C = 128
        F = 128
        N_RBF = 20
        LOG2 = float(np.log(2.0))
        Y0 = float(1.0 / np.sqrt(4.0 * np.pi))
        Y1_SCALE = float(np.sqrt(3.0 / (4.0 * np.pi)))

        def shifted_softplus(x):
            return jax.nn.softplus(x) - LOG2

        def _forward(x, idx_i, idx_j, f_ij, rcut_ij, r_ij, W_in2f_s, W_in2f_v, Wf1, bf1, Wf2, bf2, W1_s, W1_v, W2_s, W2_v):
            n = x.shape[0]
            e = r_ij.shape[0]
            xs = x[:, :C] @ (W_in2f_s / np.sqrt(C))
            xv = jnp.einsum('nci,cf->nfi', x[:, C:].reshape(n, C, 3), W_in2f_v) / np.sqrt(C)
            sj = xs[idx_j]
            vj = xv[idx_j]
            u = r_ij / jnp.linalg.norm(r_ij, axis=-1, keepdims=True)
            Yv = Y1_SCALE * u
            o0a = sj * Y0
            o0b = jnp.einsum('efi,ei->ef', vj, Yv) / np.sqrt(3.0)
            s2 = jnp.stack([o0a, o0b], axis=-1).reshape(e, 2 * F)
            ova = sj[:, :, None] * Yv[:, None, :]
            ovb = vj * Y0
            v2 = jnp.stack([ova, ovb], axis=2)
            w1 = jnp.cross(vj, Yv[:, None, :]) / np.sqrt(2.0)
            ax, ay, az = (vj[..., 0], vj[..., 1], vj[..., 2])
            bx, by, bz = (Yv[:, None, 0], Yv[:, None, 1], Yv[:, None, 2])
            t = jnp.stack([(ax * by + ay * bx) / np.sqrt(2.0), (ay * bz + az * by) / np.sqrt(2.0), (2.0 * az * bz - ax * bx - ay * by) / np.sqrt(6.0), (az * bx + ax * bz) / np.sqrt(2.0), (ax * bx - ay * by) / np.sqrt(2.0)], axis=-1)
            h = shifted_softplus(f_ij @ Wf1 + bf1)
            W = (h @ Wf2 + bf2) * rcut_ij[:, None]
            m_s = s2 * W[:, :2 * F]
            m_v = (v2.reshape(e, 2 * F, 3) * W[:, 2 * F:4 * F, None]).reshape(e, 6 * F)
            m_w = (w1 * W[:, 4 * F:5 * F, None]).reshape(e, 3 * F)
            m_t = (t * W[:, 5 * F:6 * F, None]).reshape(e, 5 * F)
            x_ij = jnp.concatenate([m_s, m_v, m_w, m_t], axis=1)
            agg = jax.ops.segment_sum(x_ij, idx_i, num_segments=n)
            S = agg[:, :2 * F] @ (W1_s / np.sqrt(2 * F))
            V = jnp.einsum('nmi,mc->nci', agg[:, 2 * F:8 * F].reshape(n, 2 * F, 3), W1_v) / np.sqrt(2 * F)
            S = shifted_softplus(S)
            S = S @ (W2_s / np.sqrt(C))
            V = jnp.einsum('nci,cd->ndi', V, W2_v) / np.sqrt(C)
            return jnp.concatenate([S, V.reshape(n, 3 * C)], axis=1)
        key = jax.random.key(seed)
        ks = jax.random.split(key, 16)
        f32 = jnp.float32
        x = jax.random.normal(ks[0], (N_ATOMS, 4 * C), f32)
        idx_i = jnp.sort(jax.random.randint(ks[1], (N_EDGES,), 0, N_ATOMS))
        idx_j = jax.random.randint(ks[2], (N_EDGES,), 0, N_ATOMS)
        f_ij = jax.random.uniform(ks[3], (N_EDGES, N_RBF), f32)
        rcut_ij = jax.random.uniform(ks[4], (N_EDGES,), f32)
        r_ij = jax.random.normal(ks[5], (N_EDGES, 3), f32)
        W_in2f_s = jax.random.normal(ks[6], (C, F), f32)
        W_in2f_v = jax.random.normal(ks[7], (C, F), f32)
        Wf1 = jax.random.normal(ks[8], (N_RBF, F), f32) / np.sqrt(N_RBF)
        bf1 = 0.1 * jax.random.normal(ks[9], (F,), f32)
        Wf2 = jax.random.normal(ks[10], (F, 6 * F), f32) / np.sqrt(F)
        bf2 = 0.1 * jax.random.normal(ks[11], (6 * F,), f32)
        W1_s = jax.random.normal(ks[12], (2 * F, C), f32)
        W1_v = jax.random.normal(ks[13], (2 * F, C), f32)
        W2_s = jax.random.normal(ks[14], (C, C), f32)
        W2_v = jax.random.normal(ks[15], (C, C), f32)
        return dict(x=x, idx_i=idx_i, idx_j=idx_j, f_ij=f_ij, rcut_ij=rcut_ij, r_ij=r_ij, W_in2f_s=W_in2f_s, W_in2f_v=W_in2f_v, Wf1=Wf1, bf1=bf1, Wf2=Wf2, bf2=bf2, W1_s=W1_s, W1_v=W1_v, W2_s=W2_s, W2_v=W2_v)
    _L3_gnn_all = _L3_gnn_setup()
    _L3_gnn_in = {k: v for k, v in _L3_gnn_all.items() if k in ('W_in2f_s', 'W_in2f_v', 'Wf1', 'bf1', 'Wf2', 'bf2', 'W1_s', 'W1_v', 'W2_s', 'W2_v')}
    del _L3_gnn_all
    return {'x': x, 'src': src, 'dst': dst, 'edge_attr_20': edge_attr_20, 'edge_attr_3': edge_attr_3, 'edge_weight': edge_weight, 'L0_gnn_W1': _L0_gnn_in['W1'], 'L0_gnn_b1': _L0_gnn_in['b1'], 'L0_gnn_W2': _L0_gnn_in['W2'], 'L0_gnn_b2': _L0_gnn_in['b2'], 'L1_gnn_W_self1': _L1_gnn_in['W_self1'], 'L1_gnn_W_neigh1': _L1_gnn_in['W_neigh1'], 'L1_gnn_b1': _L1_gnn_in['b1'], 'L1_gnn_W_self2': _L1_gnn_in['W_self2'], 'L1_gnn_W_neigh2': _L1_gnn_in['W_neigh2'], 'L1_gnn_b2': _L1_gnn_in['b2'], 'L2_gnn_W': _L2_gnn_in['W'], 'L2_gnn_bias': _L2_gnn_in['bias'], 'L3_gnn_W_in2f_s': _L3_gnn_in['W_in2f_s'], 'L3_gnn_W_in2f_v': _L3_gnn_in['W_in2f_v'], 'L3_gnn_Wf1': _L3_gnn_in['Wf1'], 'L3_gnn_bf1': _L3_gnn_in['bf1'], 'L3_gnn_Wf2': _L3_gnn_in['Wf2'], 'L3_gnn_bf2': _L3_gnn_in['bf2'], 'L3_gnn_W1_s': _L3_gnn_in['W1_s'], 'L3_gnn_W1_v': _L3_gnn_in['W1_v'], 'L3_gnn_W2_s': _L3_gnn_in['W2_s'], 'L3_gnn_W2_v': _L3_gnn_in['W2_v']}

def reference(x, src, dst, edge_attr_20, edge_attr_3, edge_weight, L0_gnn_W1, L0_gnn_b1, L0_gnn_W2, L0_gnn_b2, L1_gnn_W_self1, L1_gnn_W_neigh1, L1_gnn_b1, L1_gnn_W_self2, L1_gnn_W_neigh2, L1_gnn_b2, L2_gnn_W, L2_gnn_bias, L3_gnn_W_in2f_s, L3_gnn_W_in2f_v, L3_gnn_Wf1, L3_gnn_bf1, L3_gnn_Wf2, L3_gnn_bf2, L3_gnn_W1_s, L3_gnn_W1_v, L3_gnn_W2_s, L3_gnn_W2_v):
    import jax
    import jax.numpy as jnp

    def _L0_gnn_ref(x, edge_index, W1, b1, W2, b2):
        import jax, jax.numpy as jnp
        import numpy as np
        N_NODES = 1250
        eps = 0.0
        src, dst = (edge_index[0], edge_index[1])
        agg = jax.ops.segment_sum(x[src], dst, num_segments=N_NODES)
        h = (1.0 + eps) * x + agg
        h = jax.nn.relu(h @ W1 + b1)
        out = h @ W2 + b2
        return out

    def _L1_gnn_ref(feats, src, dst, W_self1, W_neigh1, b1, W_self2, W_neigh2, b2):
        import jax, jax.numpy as jnp
        import numpy as np
        N, E, D = (625, 10000, 512)

        def _sage_layer(h, src, dst, W_self, W_neigh, b, n_nodes):
            agg = jax.ops.segment_sum(h[src], dst, num_segments=n_nodes)
            deg = jax.ops.segment_sum(jnp.ones_like(dst, dtype=h.dtype), dst, num_segments=n_nodes)
            h_neigh = agg / jnp.maximum(deg, 1.0)[:, None]
            return jax.nn.relu(h @ W_self + h_neigh @ W_neigh + b)
        n_nodes = feats.shape[0]
        h = _sage_layer(feats, src, dst, W_self1, W_neigh1, b1, n_nodes)
        h = _sage_layer(h, src, dst, W_self2, W_neigh2, b2, n_nodes)
        return h

    def _L2_gnn_ref(X, W, bias, edge_weight, edge_src, edge_dst):
        import jax, jax.numpy as jnp
        import numpy as np
        N_NODES = 3125
        N_EDGES = 100000
        D_FEAT = 512
        UNITS = 512
        h = jnp.matmul(X, W)
        msgs = h[edge_src] * edge_weight[:, None]
        agg = jax.ops.segment_sum(msgs, edge_dst, num_segments=X.shape[0])
        return jax.nn.relu(agg + bias)

    def _L3_gnn_ref(x, idx_i, idx_j, f_ij, rcut_ij, r_ij, W_in2f_s, W_in2f_v, Wf1, bf1, Wf2, bf2, W1_s, W1_v, W2_s, W2_v):
        import jax, jax.numpy as jnp
        import numpy as np
        N_ATOMS = 5000
        N_EDGES = 3125
        C = 128
        F = 128
        N_RBF = 20
        LOG2 = float(np.log(2.0))
        Y0 = float(1.0 / np.sqrt(4.0 * np.pi))
        Y1_SCALE = float(np.sqrt(3.0 / (4.0 * np.pi)))

        def shifted_softplus(x):
            return jax.nn.softplus(x) - LOG2

        def _forward(x, idx_i, idx_j, f_ij, rcut_ij, r_ij, W_in2f_s, W_in2f_v, Wf1, bf1, Wf2, bf2, W1_s, W1_v, W2_s, W2_v):
            n = x.shape[0]
            e = r_ij.shape[0]
            xs = x[:, :C] @ (W_in2f_s / np.sqrt(C))
            xv = jnp.einsum('nci,cf->nfi', x[:, C:].reshape(n, C, 3), W_in2f_v) / np.sqrt(C)
            sj = xs[idx_j]
            vj = xv[idx_j]
            u = r_ij / jnp.linalg.norm(r_ij, axis=-1, keepdims=True)
            Yv = Y1_SCALE * u
            o0a = sj * Y0
            o0b = jnp.einsum('efi,ei->ef', vj, Yv) / np.sqrt(3.0)
            s2 = jnp.stack([o0a, o0b], axis=-1).reshape(e, 2 * F)
            ova = sj[:, :, None] * Yv[:, None, :]
            ovb = vj * Y0
            v2 = jnp.stack([ova, ovb], axis=2)
            w1 = jnp.cross(vj, Yv[:, None, :]) / np.sqrt(2.0)
            ax, ay, az = (vj[..., 0], vj[..., 1], vj[..., 2])
            bx, by, bz = (Yv[:, None, 0], Yv[:, None, 1], Yv[:, None, 2])
            t = jnp.stack([(ax * by + ay * bx) / np.sqrt(2.0), (ay * bz + az * by) / np.sqrt(2.0), (2.0 * az * bz - ax * bx - ay * by) / np.sqrt(6.0), (az * bx + ax * bz) / np.sqrt(2.0), (ax * bx - ay * by) / np.sqrt(2.0)], axis=-1)
            h = shifted_softplus(f_ij @ Wf1 + bf1)
            W = (h @ Wf2 + bf2) * rcut_ij[:, None]
            m_s = s2 * W[:, :2 * F]
            m_v = (v2.reshape(e, 2 * F, 3) * W[:, 2 * F:4 * F, None]).reshape(e, 6 * F)
            m_w = (w1 * W[:, 4 * F:5 * F, None]).reshape(e, 3 * F)
            m_t = (t * W[:, 5 * F:6 * F, None]).reshape(e, 5 * F)
            x_ij = jnp.concatenate([m_s, m_v, m_w, m_t], axis=1)
            agg = jax.ops.segment_sum(x_ij, idx_i, num_segments=n)
            S = agg[:, :2 * F] @ (W1_s / np.sqrt(2 * F))
            V = jnp.einsum('nmi,mc->nci', agg[:, 2 * F:8 * F].reshape(n, 2 * F, 3), W1_v) / np.sqrt(2 * F)
            S = shifted_softplus(S)
            S = S @ (W2_s / np.sqrt(C))
            V = jnp.einsum('nci,cd->ndi', V, W2_v) / np.sqrt(C)
            return jnp.concatenate([S, V.reshape(n, 3 * C)], axis=1)
        return _forward(x, idx_i, idx_j, f_ij, rcut_ij, r_ij, W_in2f_s, W_in2f_v, Wf1, bf1, Wf2, bf2, W1_s, W1_v, W2_s, W2_v)
    edge_index = jnp.stack([src, dst])
    x = _layernorm(x + _L0_gnn_ref(x, edge_index, L0_gnn_W1, L0_gnn_b1, L0_gnn_W2, L0_gnn_b2), axis=-1)
    x = _layernorm(x + _L1_gnn_ref(x, src, dst, L1_gnn_W_self1, L1_gnn_W_neigh1, L1_gnn_b1, L1_gnn_W_self2, L1_gnn_W_neigh2, L1_gnn_b2), axis=-1)
    x = _layernorm(x + _L2_gnn_ref(x, L2_gnn_W, L2_gnn_bias, edge_weight, src, dst), axis=-1)
    x = _layernorm(x + _L3_gnn_ref(x, src, dst, edge_attr_20, edge_weight, edge_attr_3, L3_gnn_W_in2f_s, L3_gnn_W_in2f_v, L3_gnn_Wf1, L3_gnn_bf1, L3_gnn_Wf2, L3_gnn_bf2, L3_gnn_W1_s, L3_gnn_W1_v, L3_gnn_W2_s, L3_gnn_W2_v), axis=-1)
    return x

_drawn_inputs = setup_inputs


def setup_inputs(seed=0):
    import zlib

    import numpy as np

    out = dict(_drawn_inputs(seed))
    spreads = {'L1_gnn_b1': (0.0, 0.1), 'L1_gnn_b2': (0.0, 0.1), 'L2_gnn_bias': (0.0, 0.548)}
    factors = {'L0_gnn_b1': 6.606}
    for name, (base, spread) in spreads.items():
        noise = np.random.default_rng([zlib.crc32(name.encode()), seed]).standard_normal(out[name].shape)
        drawn = base * np.exp(spread * noise) if base else spread * noise
        out[name] = jnp.asarray(drawn.astype(out[name].dtype))
    for name, factor in factors.items():
        out[name] = (out[name] * factor).astype(out[name].dtype)
    return out
```

```python
import math
from contextlib import ExitStack

import numpy as np
import concourse.bass as bass
from concourse import mybir

P = 128
N, D, E = 1250, 512, 40000
NT = (N + P - 1) // P
TAIL = N - (NT - 1) * P
KT = D // P
PIECES = [(0, 512), (512, 512), (1024, N - 1024)]

EP, EJ = 125, 320
LT = 4
LJ = EJ // LT

BUCKETS = [NT * NT, NT]
QUANT_LOG2 = [7, 9]
LOTS_PER_BANK = [5, 40]
PAIR_CHUNKS = 4 * math.ceil((E + BUCKETS[0] * (P - 1)) // P / 4)
GROUP = 4
GROUPS = (E + NT * (GROUP * P - 1)) // (GROUP * P)
GROUPS += GROUPS % 2
SRC_CHUNKS = GROUPS * GROUP
CHUNKS = [PAIR_CHUNKS, SRC_CHUNKS]
PAIR_COLS, SRC_COLS = 4, 32

C_ONE, C_Y, C_R, C_SRC, C_DST = 20, 21, 24, 25, 26

AW_COLS = (NT - 1) * N + NT * P
MSG = 8 * P

LOG2 = float(np.log(2.0))
Y0 = float(1.0 / np.sqrt(4.0 * np.pi))
Y1_SCALE = float(np.sqrt(3.0 / (4.0 * np.pi)))
EPS = 1e-5

STAGES = [("l0_agg", 12), ("l0_up", 12), ("l0_down", NT),
          ("l1_xT", NT), ("deg", 3), ("l1a_agg", 12), ("l1a_out", NT),
          ("l1b_xT", NT), ("l1b_agg", 12), ("l1b_out", NT),
          ("l2_xT", NT), ("l2_h", NT), ("l2_agg", NT), ("l3_xT", NT), ("l3_z", NT)]
NB = 8


def build(nc, x, src, dst, edge_attr_20, edge_attr_3, edge_weight,
          l0_w1, l0_b1, l0_w2, l0_b2, l1_ws1, l1_wn1, l1_b1, l1_ws2, l1_wn2, l1_b2,
          l2_w, l2_b, w_in_s, w_in_v, wf1, bf1, wf2, bf2, w1_s, w1_v, w2_s, w2_v, out):
    f32, bf16, i32, u32 = mybir.dt.float32, mybir.dt.bfloat16, mybir.dt.int32, mybir.dt.uint32
    ALU, ACT, AX = mybir.AluOpType, mybir.ActivationFunctionType, mybir.AxisListType
    ds = bass.ds

    tables = [nc.dram_tensor("pair_table", [P * PAIR_CHUNKS, PAIR_COLS], f32, kind="Internal").ap(),
              nc.dram_tensor("src_table", [P * SRC_CHUNKS, SRC_COLS], f32, kind="Internal").ap()]
    records = nc.dram_tensor("records", [EP, EJ * SRC_COLS], f32, kind="Internal").ap()
    z_table = nc.dram_tensor("z_table", [N, D], f32, kind="Internal").ap()

    ctx = ExitStack()
    with ctx:
        def sb(name, shape, dt=f32):
            return ctx.enter_context(nc.sbuf_tensor(name, shape, dt))

        def sem(name):
            return ctx.enter_context(nc.semaphore(name))

        adj_t = sb("adj_t", [P, 2 * AW_COLS])
        adj = adj_t[:, :].rearrange("p (k n) -> p k n", k=2)
        dense = sb("dense", [P, NT * D + 2 * KT * N])
        xb = dense[:, 0:NT * D].rearrange("p (t n) -> p t n", t=NT)
        T1 = dense[:, NT * D:NT * D + KT * N].rearrange("p (k n) -> p k n", k=KT)
        T2 = dense[:, NT * D + KT * N:NT * D + 2 * KT * N].rearrange("p (k n) -> p k n", k=KT)
        xa_t = sb("xa", [P, NT * D])
        xa = xa_t[:, :].rearrange("p (t n) -> p t n", t=NT)
        wring = sb("wring", [P, 2, KT, D])
        shared = sb("shared", [P, N + D])
        pair_sb = shared[:, 0:PAIR_CHUNKS * PAIR_COLS].rearrange("p (c w) -> p c w", w=PAIR_COLS)
        rdeg = shared[:, 0:N]
        bias_sb = shared[:, N:N + D]
        iota = sb("iota", [P, P])
        ident = sb("ident", [P, P])
        identb = sb("identb", [P, P], bf16)
        onesb = sb("onesb", [P, P], bf16)
        trib = sb("trib", [P, P], bf16)
        window = sb("window", [P, 2 * LJ], bf16)
        ones_f = sb("ones_f", [P, P])
        pcol = sb("pcol", [P, 1])
        ybuf = sb("ybuf", [P, D])
        rows_i = [dense[:, 14576:14576 + EJ].bitcast(i32), sb("src_rows", [P, EJ], i32)[:, :]]
        offs = [ybuf[0:1, 0:PAIR_CHUNKS].bitcast(i32), sb("src_offs", [1, P], i32)[:, :]]
        b1col = sb("b1col", [P, KT])
        lnt = sb("lnt", [P, 12])

        at = [0]

        def carve(parts, n, dt=f32):
            words = n if dt != bf16 else (n + 1) // 2
            v = adj_t[0:parts, at[0]:at[0] + words]
            at[0] += words
            return v if dt == f32 else v.bitcast(dt)

        ind = [carve(EP, EJ * b, bf16).rearrange("p (j b) -> p j b", b=b) for b in BUCKETS]
        src_i, dst_i, tmp_i, tmp2_i = [carve(EP, EJ, i32) for _ in range(4)]
        src_tile, dst_tile, tmp_f, weight_f = [carve(EP, EJ) for _ in range(4)]
        keys = [carve(EP, EJ), src_tile]
        pos_f = carve(EP, EJ)
        xyz = carve(EP, 3 * EJ).rearrange("p (j i) -> p j i", i=3)
        prod_w = max(LOTS_PER_BANK[s] * BUCKETS[s] for s in range(2))
        prod = [carve(EP, prod_w) for _ in range(2)]
        zeros_w = carve(P, 400, bf16)
        cnt_sb = carve(P, LT * BUCKETS[0], bf16)
        base_f = carve(P, LT * BUCKETS[0])
        base_i = carve(P, LT * BUCKETS[0], i32)
        base_hi = carve(P, LT * BUCKETS[0], bf16)
        base_lo = carve(P, LT * BUCKETS[0], bf16)
        nch_i, end_c, start_c, step_w, cmp_w, nch_f = [carve(P, BUCKETS[0], i32 if k == 0 else f32) for k in range(6)]
        offcol = carve(P, 4)
        chunk_no = carve(P, 4)
        fill = dense[:, 12928:12928 + PAIR_CHUNKS * PAIR_COLS]
        assert at[0] <= 2 * AW_COLS
        rec0 = dense[0:EP, 0:EJ * SRC_COLS].rearrange("p (j w) -> p j w", w=SRC_COLS)
        pair_rec = dense[0:EP, EJ * SRC_COLS:EJ * (SRC_COLS + PAIR_COLS)].rearrange("p (j w) -> p j w", w=PAIR_COLS)
        attr_half = wring[0:EP, :, :, :].rearrange("p a b c -> p (a b c)")[:, 0:EJ // 2 * 20].rearrange("p (j w) -> p j w", w=20)
        fill32 = dense[:, EJ * (SRC_COLS + PAIR_COLS):EJ * (SRC_COLS + PAIR_COLS) + 44 * SRC_COLS].rearrange("p (c w) -> p c w", w=SRC_COLS)

        st_idx = sb("st_idx", [P, 2, 4], i32)
        st_rec = sb("st_rec", [P, 2, 4 * SRC_COLS])

        AB = 4
        sel_s = dense[:, 0:AB * P].rearrange("p (c n) -> p c n", n=P)
        sel_d = dense[:, AB * P:3 * AB * P].rearrange("p (c k n) -> p c k n", k=2, n=P)

        at[0] = 0
        agg = carve(P, NT * MSG)
        zg = carve(P, 2 * GROUP * D).rearrange("p (s c n) -> p s c n", s=2, c=GROUP)
        recg = carve(P, 2 * GROUP * SRC_COLS).rearrange("p (s c w) -> p s c w", s=2, c=GROUP)
        dsti = carve(P, 2 * GROUP, i32).rearrange("p (s c) -> p s c", s=2)
        msg = carve(P, GROUP * (MSG + P)).rearrange("p (c n) -> p c n", c=GROUP)
        hT = carve(P, 2 * D).rearrange("p (s n) -> p s n", s=2)
        fT = carve(SRC_COLS, 2 * D).rearrange("p (s n) -> p s n", s=2)
        sp = carve(P, D)
        vy = carve(P, GROUP * P).rearrange("p (c n) -> p c n", c=GROUP)
        oh = carve(P, GROUP * P).rearrange("p (c n) -> p c n", c=GROUP)
        aT = carve(P, 2 * MSG).rearrange("p (s m n) -> p s m n", s=2, m=8)
        svT = T1[:, 1, 0:2 * D].rearrange("p (s n) -> p s n", s=2)
        assert at[0] <= 2 * AW_COLS
        wl = wring[:, :, :, :].rearrange("p a b c -> p (a b c)")
        wl_at = [0]

        def wcarve(parts, n, dt=f32):
            words = n if dt != bf16 else n // 2
            v = wl[0:parts, wl_at[0]:wl_at[0] + words]
            wl_at[0] += words
            return v if dt == f32 else v.bitcast(dt)

        in_w = wcarve(P, 2 * P).rearrange("p (k n) -> p k n", k=2)
        w1s = wcarve(P, 2 * P).rearrange("p (k n) -> p k n", k=2)
        w1v = wcarve(P, 2 * P).rearrange("p (k n) -> p k n", k=2)
        w2sv = wcarve(P, 2 * P).rearrange("p (k n) -> p k n", k=2)
        wf1_sb = wcarve(SRC_COLS, P)
        wf2_sb = wcarve(P, D)
        bf2_f = wcarve(3, D)
        bf2_t = wcarve(3, D)
        bf2_b = wcarve(3, D, bf16)
        bf2_p = wcarve(3, D, bf16)
        half_t = wcarve(P, 1)
        stat = ybuf[:, 0:2 * NT].rearrange("p (k t) -> p k t", k=2)
        vprod = T1[:, 2, 0:3 * P].rearrange("p (k n) -> p k n", k=3)
        wf2_raw = T1[:, 0, 0:D]

        ps = [ctx.enter_context(nc.psum_tensor(f"ps{i}", [P, 512], f32)) for i in range(6)]
        ps67 = ctx.enter_context(nc.psum_tensor("ps67", [P, 1024], f32))
        bank = [ps[i][:, :] for i in range(6)] + [ps67[:, 0:512], ps67[:, 512:1024]]

        edges_in, weight_in, xyz_in, x_in = sem("edges_in"), sem("weight_in"), sem("xyz_in"), sem("x_in")
        attr_in, attr_used = sem("attr_in"), sem("attr_used")
        consts = sem("consts")
        filled, rec_out = sem("filled"), sem("rec_out")
        fill_ready = sem("fill_ready")
        recs_ready = sem("recs_ready")
        ind_ready = [sem(f"ind_ready{s}") for s in range(2)]
        cnt_done = [sem(f"cnt_done{s}") for s in range(2)]
        cnt_sb_ready = [sem(f"cnt_sb_ready{s}") for s in range(2)]
        base_done = [sem(f"base_done{s}") for s in range(2)]
        base_ready = [sem(f"base_ready{s}") for s in range(2)]
        pos_done = [sem(f"pos_done{s}") for s in range(2)]
        pos_read = [sem(f"pos_read{s}") for s in range(2)]
        off_done = [sem(f"off_done{s}") for s in range(2)]
        rows_ready = [sem(f"rows_ready{s}") for s in range(2)]
        offs_ready = [sem(f"offs_ready{s}") for s in range(2)]
        tick = sem("tick")
        chain = sem("chain")
        gchain = sem("gchain")
        achain = sem("achain")
        staged = [sem(f"staged{s}") for s in range(2)]
        scat = [[sem(f"scat{s}{k}") for k in range(2)] for s in range(2)]
        st_load = [sem(f"st_load{k}") for k in range(2)]
        pair_in = sem("pair_in")
        sq_ready, norm_ready = sem("sq_ready"), sem("norm_ready")
        var_ready, std_ready = sem("var_ready"), sem("std_ready")
        pair_rec_ready = sem("pair_rec_ready")
        ones_ready = sem("ones_ready")
        pos_step = [sem(f"pos_step{s}") for s in range(2)]
        offs_read = sem("offs_read")
        sel_ready, sel_used = sem("sel_ready"), sem("sel_used")
        selw_ready = sem("selw_ready")
        blk_done, blk_added = sem("blk_done"), sem("blk_added")
        full = sem("full")
        done = {name: sem("done_" + name) for name, _ in STAGES}
        w_in = [sem(f"w_in{k}") for k in range(2)]
        bias_in, b1_in = sem("bias_in"), sem("b1_in")
        z_out = sem("z_out")
        l3w_in, l3w_ready = sem("l3w_in"), sem("l3w_ready")
        in_w_ready = sem("in_w_ready")
        rec_in = [sem(f"rec_in{k}") for k in range(2)]
        z_in = [sem(f"z_in{k}") for k in range(GROUP)]
        dsti_ready = sem("dsti_ready")
        fT_done, fT_ready, u_done, sp_ready, h_ready = sem("fT_done"), sem("fT_ready"), sem("u_done"), sem("sp_ready"), sem("h_ready")
        sp_chain = sem("sp_chain")
        vy_ready, vy_chain = sem("vy_ready"), sem("vy_chain")
        oh_ready = sem("oh_ready")
        filt_done, msg_a, msg_ready, cmul_ready = sem("filt_done"), sem("msg_a"), sem("msg_ready"), sem("cmul_ready")
        scat_chunk = sem("scat_chunk")
        agg_added = sem("agg_added")
        agg_zero = sem("agg_zero")
        t_done, aT_ready, sv_done, svT_ready, o_done, o_read = sem("t_done"), sem("aT_ready"), sem("sv_done"), sem("svT_ready"), sem("o_done"), sem("o_read")
        act_sv = sem("act_sv")
        y_ready, out_done = sem("y_ready"), sem("out_done")

        def wait_alone(eng, s, value):
            eng.wait_ge(s, value).then_inc(tick, 1)

        class Chain:
            def __init__(self, eng, s):
                self.eng, self.s, self.n = eng, s, 0

            def __call__(self, ins):
                self.n += 1
                ins.then_inc(self.s, 1)
                self.eng.wait_ge(self.s, self.n)

        first = {}
        total = 0
        for name, count in STAGES:
            first[name] = total
            total += count
        place = [(name, k) for name, count in STAGES for k in range(count)]

        def rows_of(t):
            return P if t < NT - 1 else TAIL

        SCAT_IT = EJ // 8
        AB_IT = PAIR_CHUNKS // AB
        L3_IT = GROUPS // 2

        block = ctx.enter_context(nc.Block())

        @block.sync
        def _(sp_eng):
            sp_eng.dma_start(src_i, src.rearrange("(p j) -> p j", p=EP)).then_inc(edges_in, 16)
            sp_eng.dma_start(dst_i, dst.rearrange("(p j) -> p j", p=EP)).then_inc(edges_in, 16)
            sp_eng.wait_ge(fill_ready, 2)
            sp_eng.dma_start(tables[0].rearrange("(p c) w -> p (c w)", p=P), fill).then_inc(filled, 16)
            t1 = tables[1].rearrange("(p c) w -> p c w", p=P)
            for c in range(0, SRC_CHUNKS, 44):
                sp_eng.dma_start(t1[:, c:c + 44, :], fill32).then_inc(filled, 16)
            sp_eng.dma_start(xyz, edge_attr_3.rearrange("(p j) i -> p j i", p=EP)).then_inc(xyz_in, 16)
            attr = edge_attr_20.rearrange("(p j) w -> p j w", p=EP)
            for h in range(2):
                if h:
                    sp_eng.wait_ge(attr_used, h)
                sp_eng.dma_start(attr_half, attr[:, h * (EJ // 2):(h + 1) * (EJ // 2), :]).then_inc(attr_in, 16)
            sp_eng.wait_ge(x_in, 1)
            sp_eng.dma_start(xa[:, 0:NT - 1, :], x[0:(NT - 1) * P, :].rearrange("(t p) n -> p t n", p=P)).then_inc(x_in, 16)
            sp_eng.dma_start(xa[0:TAIL, NT - 1, :], x[(NT - 1) * P:N, :]).then_inc(x_in, 16)
            sp_eng.wait_ge(recs_ready, 3)
            sp_eng.dma_start(records, rec0.rearrange("p j w -> p (j w)")).then_inc(rec_out, 16)
            sp_eng.dma_start(b1col[:, :], l0_b1.rearrange("(m p) -> p m", p=P), allow_slow_non_contiguous=True).then_inc(b1_in, 16)
            ring = [(l0_w1, None), (l0_w2, None), (l1_ws1, "l0_up"), (l1_wn1, "l0_down"),
                    (l1_ws2, "l1a_out"), (l1_wn2, "l1a_out"), (l2_w, "l1b_out")]
            sp_eng.wait_ge(attr_used, 2)
            biases = {1: (l0_b2, None), 3: (l1_b1, "l0_down"), 5: (l1_b2, "l1a_out"), 6: (l2_b, "l1b_out")}
            for q, (w, after) in enumerate(ring):
                if after:
                    sp_eng.wait_ge(full, first[after] + dict(STAGES)[after])
                sp_eng.dma_start(wring[:, q % 2, :, :], w.rearrange("(t k) n -> k t n", k=P)).then_inc(w_in[q % 2], 16)
                if q == 1:
                    for k in range(2):
                        sp_eng.wait_ge(scat[0][k], 16 * 4 * SCAT_IT)
                    sp_eng.dma_start(pair_sb.rearrange("p c w -> p (c w)"),
                                     tables[0].rearrange("(p c) w -> p (c w)", p=P)).then_inc(pair_in, 16)
                    sp_eng.wait_ge(blk_added, PAIR_CHUNKS)
                if q in biases:
                    b, after = biases[q]
                    if after:
                        sp_eng.wait_ge(done[after], NT)
                    sp_eng.dma_start(bias_sb, b.partition_broadcast(P)).then_inc(bias_in, 16)
            sp_eng.wait_ge(full, first["l2_h"] + NT)
            sp_eng.wait_ge(l3w_ready, 1)
            loads = [(in_w[:, 0, :], w_in_s), (in_w[:, 1, :], w_in_v),
                     (w1s, w1_s.rearrange("(f k) c -> f k c", k=2)), (w1v, w1_v.rearrange("(f k) c -> f k c", k=2)),
                     (w2sv[:, 0, :], w2_s), (w2sv[:, 1, :], w2_v), (wf1_sb[0:20, :], wf1),
                     (wf1_sb[20:21, :], bf1.rearrange("(a n) -> a n", a=1)), (bf2_t, bf2[0:D].partition_broadcast(3)),
                     (wf2_raw, wf2[:, 0:D])]
            for o, i in loads:
                sp_eng.dma_start(o, i).then_inc(l3w_in, 16)

            tsrc = tables[1].rearrange("(p c) w -> p (c w)", p=P)

            def load_group(i, s):
                g = 2 * i + s
                if not isinstance(i, int) or i > 0:
                    wait_alone(sp_eng, fT_done, g - 1)
                    wait_alone(sp_eng, vy_ready, GROUP * (g - 1))
                    wait_alone(sp_eng, oh_ready, GROUP * (g - 1))
                    wait_alone(sp_eng, cmul_ready, GROUP * (g - 1))
                sp_eng.dma_start(recg[:, s, :, :].rearrange("p c w -> p (c w)"),
                                 tsrc[:, ds(g * (GROUP * SRC_COLS), GROUP * SRC_COLS)]).then_inc(rec_in[s], 16)

            for k in range(2):
                sp_eng.wait_ge(scat[1][k], 16 * 4 * SCAT_IT)
            sp_eng.wait_ge(full, first["l2_agg"] + NT)
            load_group(0, 0)
            load_group(0, 1)
            with sp_eng.Fori(1, L3_IT) as i:
                load_group(i, 0)
                load_group(i, 1)

        @block.gpsimd
        def _(pool):
            g = nc.gpsimd
            link = Chain(pool, gchain)
            link(g.memset(window[:, :], 0.0))
            g.memset(window[:, LJ - 1:LJ], 1.0).then_inc(consts, 1)
            g.memset(onesb[:, :], 1.0).then_inc(consts, 1)
            g.memset(zeros_w, 0.0).then_inc(consts, 1)
            link(g.iota(iota[:, :], [[1, P]], base=0, channel_multiplier=0, allow_small_or_imprecise_dtypes=True))
            link(g.iota(pcol[:, :], [[0, 1]], base=0, channel_multiplier=1, allow_small_or_imprecise_dtypes=True))
            g.iota(chunk_no, [[P, 4]], base=0, channel_multiplier=1, allow_small_or_imprecise_dtypes=True).then_inc(consts, 1)
            link(g.tensor_scalar(ident[:, :], iota[:, :], pcol[:, :], None, ALU.is_equal))
            g.tensor_copy(identb[:, :], ident[:, :]).then_inc(consts, 1)
            g.tensor_scalar(trib[:, :], iota[:, :], pcol[:, :], None, ALU.is_gt).then_inc(consts, 1)
            link(g.memset(fill, 0.0))
            fv = fill.rearrange("p (c w) -> p c w", w=PAIR_COLS)
            g.memset(fv[:, :, 0:2], -1.0).then_inc(fill_ready, 1)
            link(g.memset(fill32, 0.0))
            g.memset(fill32[:, :, C_SRC:C_SRC + 1], -1.0).then_inc(fill_ready, 1)
            g.memset(xa[:, NT - 1, :], 0.0).then_inc(x_in, 1)
            link(g.memset(rec0[:, :, C_DST + 1:SRC_COLS], 0.0))
            g.memset(rec0[:, :, C_ONE:C_ONE + 1], 1.0).then_inc(recs_ready, 1)

            def stage(s, i, k):
                j = i * 8 + 4 * k
                if s == 0:
                    g.tensor_copy(st_idx[0:EP, k, :], rows_i[s][0:EP, ds(j, 4)]).then_inc(staged[s], 1)
                    g.tensor_copy(st_rec[0:EP, k, 0:4 * PAIR_COLS],
                                  dense[0:EP, ds(j * PAIR_COLS + EJ * SRC_COLS, 4 * PAIR_COLS)]).then_inc(staged[s], 1)
                else:
                    pool.dma_start(st_rec[0:EP, k, :], records[:, ds(j * SRC_COLS, 4 * SRC_COLS)]).then_inc(st_load[k], 16)
                    g.tensor_copy(st_idx[0:EP, k, :], rows_i[s][0:EP, ds(j, 4)]).then_inc(staged[s], 1)

            def scatter(s, i, k):
                w = (PAIR_COLS, SRC_COLS)[s]
                if s == 0:
                    wait_alone(pool, staged[s], 4 * i + 2 * k + 2)
                else:
                    wait_alone(pool, staged[s], 2 * i + k + 1)
                    wait_alone(pool, st_load[k], 16 * (i + 1))
                for c in range(4):
                    g.indirect_dma_start(out=tables[s], out_offset=bass.IndirectOffsetOnAxis(ap=st_idx[0:EP, k, c:c + 1].bitcast(u32), axis=0),
                                         in_=st_rec[0:EP, k, c * w:(c + 1) * w], in_offset=None).then_inc(scat[s][k], 16)

            for s in range(2):
                pool.wait_ge(rows_ready[s], 1)
                if s == 0:
                    pool.wait_ge(pair_rec_ready, 2)
                    pool.wait_ge(filled, 16 * (1 + SRC_CHUNKS // 44))
                else:
                    pool.wait_ge(rec_out, 16)
                    for k in range(2):
                        pool.wait_ge(scat[0][k], 64 * SCAT_IT)

                def turn(i):
                    for k in range(2):
                        if not isinstance(i, int) or i > 0:
                            wait_alone(pool, scat[s][k], 64 * i)
                        stage(s, i, k)
                    for k in range(2):
                        scatter(s, i, k)

                turn(0)
                with pool.Fori(1, SCAT_IT) as i:
                    turn(i)

            def gather(i, s, c):
                gi = 2 * i + s
                n = GROUP * gi + c
                if c == 0:
                    wait_alone(pool, rec_in[s], 16 * (i + 1))
                    g.tensor_copy(dsti[:, s, :], recg[:, s, :, C_DST]).then_inc(dsti_ready, 1)
                    wait_alone(pool, dsti_ready, gi + 1)
                if not (isinstance(n, int) and n < 2 * GROUP):
                    wait_alone(pool, msg_ready, n - 2 * GROUP + 1)
                g.indirect_dma_start(out=zg[:, s, c, :], out_offset=None, in_=z_table,
                                     in_offset=bass.IndirectOffsetOnAxis(ap=dsti[:, s, c:c + 1].bitcast(u32), axis=0)).then_inc(z_in[c], 16)

            def vdoty(i, s, c):
                gi = 2 * i + s
                n = GROUP * gi + c
                wait_alone(pool, z_in[c], 16 * (gi + 1))
                if not (isinstance(n, int) and n < GROUP):
                    wait_alone(pool, msg_ready, n - GROUP + 1)
                y = recg[:, s, c, C_Y:C_Y + 3].unsqueeze(2).to_broadcast([P, 3, P])
                if not (isinstance(n, int) and n == 0):
                    wait_alone(pool, vy_ready, n)
                g.tensor_tensor(vprod, zg[:, s, c, P:4 * P].rearrange("p (k n) -> p k n", k=3), y, ALU.mult).then_inc(vy_chain, 1)
                wait_alone(pool, vy_chain, 2 * n + 1)
                g.tensor_tensor(vy[:, c, :], vprod[:, 0, :], vprod[:, 1, :], ALU.add).then_inc(vy_chain, 1)
                wait_alone(pool, vy_chain, 2 * n + 2)
                g.tensor_tensor(vy[:, c, :], vy[:, c, :], vprod[:, 2, :], ALU.add).then_inc(vy_ready, 1)

            def group(i, s, tail=False):
                nxt = (i, 1) if s == 0 else (i + 1, 0)
                for c in range(GROUP):
                    vdoty(i, s, c)
                    if c < 2:
                        gather(i, s, c + 2)
                    elif not tail:
                        gather(*nxt, c - 2)

            pool.wait_ge(z_out, 16 * NT)
            gather(0, 0, 0)
            gather(0, 0, 1)
            group(0, 0)
            group(0, 1)
            with pool.Fori(1, L3_IT - 1) as i:
                group(i, 0)
                group(i, 1)
            group(L3_IT - 1, 0)
            group(L3_IT - 1, 1, tail=True)

        @block.tensor
        def _(pe):
            mm = nc.tensor.matmul
            pe.wait_ge(consts, 6)
            for s in range(2):
                B, L = BUCKETS[s], LOTS_PER_BANK[s]
                W = LT * B
                mm(bank[0][0:LJ, 0:W], zeros_w[0:EP, 0:LJ], zeros_w[0:EP, 0:W], start=True, stop=False)
                for t in range(LT):
                    pe.wait_ge(ind_ready[s], t + 1)
                    with pe.Fori(0, LJ // 8) as i:
                        for u in range(8):
                            mm(bank[0][0:LJ, t * B:(t + 1) * B], window[0:EP, ds(LJ - 1 - u - i * 8, LJ)],
                               ind[s][:, ds(i * 8 + (t * LJ + u), 1), :].rearrange("p a b -> p (a b)"), start=False, stop=False)
                mm(bank[0][0:LJ, 0:W], zeros_w[0:EP, 0:LJ], zeros_w[0:EP, 0:W], start=False, stop=True).then_inc(cnt_done[s], 1)
                pe.wait_ge(cnt_sb_ready[s], 1)
                for t in range(LT):
                    for t2 in range(t + 1):
                        lhs = trib if t2 == t else onesb
                        mm(bank[1][0:LJ, t * B:(t + 1) * B], lhs[0:LJ, 0:LJ], cnt_sb[0:LJ, t2 * B:(t2 + 1) * B],
                           start=t2 == 0, stop=t2 == t)
                for t in range(LT):
                    last = mm(bank[2][:, 0:B], onesb[0:LJ, :], cnt_sb[0:LJ, t * B:(t + 1) * B], start=t == 0, stop=t == LT - 1)
                last.then_inc(base_done[s], 1)
                pe.wait_ge(base_ready[s], 1)
                nb = LJ // L
                for t in range(LT):
                    def ranks(i, u):
                        b = 4 + u
                        n = t * nb + i * 2 + u
                        if not (isinstance(i, int) and n < 2):
                            pe.wait_ge(pos_read[s], n - 1)
                        j = (i * 2 + u) * L
                        mm(bank[b][0:EP, 0:L * B], trib[0:EP, 0:EP],
                           ind[s][:, ds(j + t * LJ, L), :].rearrange("p a b -> p (a b)"), start=True, stop=False)
                        for c in range(L):
                            col = identb[0:LJ, ds(j + c, 1)].to_broadcast([LJ, EP])
                            mm(bank[b][0:EP, c * B:(c + 1) * B], col, base_hi[0:LJ, t * B:(t + 1) * B], start=False, stop=False)
                            last = mm(bank[b][0:EP, c * B:(c + 1) * B], col, base_lo[0:LJ, t * B:(t + 1) * B], start=False, stop=c == L - 1)
                        last.then_inc(pos_done[s], 1)
                    if t == 0 or nb == 2:
                        for u in range(2):
                            ranks(0, u)
                    if nb > 2:
                        with pe.Fori(1 if t == 0 else 0, nb // 2) as i:
                            for u in range(2):
                                ranks(i, u)
                tiles = math.ceil((PAIR_CHUNKS, GROUPS)[s] / P)
                pe.wait_ge(offs_ready[s], tiles)
                for t in range(tiles):
                    last = mm(bank[3][0:1, t * P:(t + 1) * P], offcol[:, t:t + 1], ident[:, :], start=True, stop=True)
                last.then_inc(off_done[s], 1)

            def blocks(i):
                for c in range(AB):
                    n = i * AB + c
                    pe.wait_ge(sel_ready, n + 1)
                    pe.wait_ge(selw_ready, n + 1)
                    if not (isinstance(i, int) and i == 0):
                        pe.wait_ge(blk_added, n - AB + 1)
                    mm(bank[c][:, 0:2 * P], sel_s[:, c, :], sel_d[:, c, :, :].rearrange("p k n -> p (k n)"),
                       start=True, stop=True).then_inc(blk_done, 1)

            pe.wait_ge(offs_read, 1)
            blocks(0)
            with pe.Fori(1, AB_IT) as i:
                blocks(i)

            def bank_for(name, k):
                n = first[name] + k
                if n >= NB:
                    before, kb = place[n - NB]
                    pe.wait_ge(done[before], kb + 1)
                return bank[n % NB]

            def agg_T(name, feats, ready, k_of):
                for m in range(KT):
                    for q, (c0, w) in enumerate(PIECES):
                        b = bank_for(name, m * 3 + q)
                        for t in range(NT):
                            if m == 0 and q == 0 and ready is not None:
                                pe.wait_ge(ready, t + 1)
                            last = mm(b[:, 0:w], feats[:, t, m * P:(m + 1) * P], adj[:, k_of, t * N + c0:t * N + c0 + w],
                                      start=t == 0, stop=t == NT - 1 and name != "l0_agg")
                        if name == "l0_agg":
                            tiles = [t for t in range(NT) if c0 <= t * P < c0 + w]
                            for t in tiles:
                                r = rows_of(t)
                                last = mm(b[:, t * P - c0:t * P - c0 + r], feats[:, t, m * P:(m + 1) * P], ident[:, 0:r],
                                          start=False, stop=t == tiles[-1])
                        last.then_inc(full, 1)

            def transposed(name, feats, ready):
                for t in range(NT):
                    b, r = bank_for(name, t), rows_of(t)
                    pe.wait_ge(ready, t + 1)
                    for m in range(KT):
                        last = nc.tensor.transpose(b[:, m * P:m * P + r], feats[0:r, t, m * P:(m + 1) * P], ident[0:r, 0:r])
                    last.then_inc(full, 1)

            def rows_product(name, parts):
                for t in range(NT):
                    b, r = bank_for(name, t), rows_of(t)
                    for a, (lhs, w) in enumerate(parts):
                        for k in range(KT):
                            last = mm(b[0:r, :], lhs[:, k, t * P:t * P + r], w[:, k, :], start=a == 0 and k == 0,
                                      stop=a == len(parts) - 1 and k == KT - 1)
                    last.then_inc(full, 1)

            w0, w1 = wring[:, 0, :, :], wring[:, 1, :, :]
            pe.wait_ge(blk_added, PAIR_CHUNKS)
            pe.wait_ge(x_in, 33)
            agg_T("l0_agg", xa, None, 0)
            pe.wait_ge(w_in[0], 16)
            pe.wait_ge(done["l0_agg"], 12)
            for m in range(KT):
                for q, (c0, w) in enumerate(PIECES):
                    b = bank_for("l0_up", m * 3 + q)
                    for k in range(KT):
                        last = mm(b[:, 0:w], w0[:, k, m * P:(m + 1) * P], T1[:, k, c0:c0 + w], start=k == 0, stop=k == KT - 1)
                    last.then_inc(full, 1)
            pe.wait_ge(w_in[1], 16)
            pe.wait_ge(done["l0_up"], 12)
            rows_product("l0_down", [(T2, w1)])
            transposed("l1_xT", xa, done["l0_down"])
            for q, (c0, w) in enumerate(PIECES):
                b = bank_for("deg", q)
                pe.wait_ge(ones_ready, 1)
                for t in range(NT):
                    last = mm(b[:, 0:w], ones_f[:, :], adj[:, 0, t * N + c0:t * N + c0 + w], start=t == 0, stop=t == NT - 1)
                last.then_inc(full, 1)
            agg_T("l1a_agg", xa, None, 0)
            pe.wait_ge(w_in[0], 32)
            pe.wait_ge(w_in[1], 32)
            pe.wait_ge(done["l1_xT"], NT)
            pe.wait_ge(done["l1a_agg"], 12)
            rows_product("l1a_out", [(T2, w0), (T1, w1)])
            transposed("l1b_xT", xb, done["l1a_out"])
            agg_T("l1b_agg", xb, None, 0)
            pe.wait_ge(w_in[0], 48)
            pe.wait_ge(w_in[1], 48)
            pe.wait_ge(done["l1b_xT"], NT)
            pe.wait_ge(done["l1b_agg"], 12)
            rows_product("l1b_out", [(T2, w0), (T1, w1)])
            transposed("l2_xT", xa, done["l1b_out"])
            pe.wait_ge(w_in[0], 64)
            pe.wait_ge(done["l2_xT"], NT)
            rows_product("l2_h", [(T2, w0)])
            pe.wait_ge(done["l2_h"], NT)
            for t in range(NT):
                b, r = bank_for("l2_agg", t), rows_of(t)
                for k in range(NT):
                    last = mm(b[0:r, :], adj[0:rows_of(k), 1, k * N + t * P:k * N + t * P + r], xb[0:rows_of(k), k, :],
                              start=k == 0, stop=k == NT - 1)
                last.then_inc(full, 1)
            for t in range(NT):
                b, r = bank_for("l3_xT", t), rows_of(t)
                pe.wait_ge(done["l2_agg"], t + 1)
                for m in range(KT):
                    part = xa[0:r, t, 0:P] if m == 0 else xa[0:r, t, P + m - 1:D:3]
                    last = nc.tensor.transpose(b[:, m * P:m * P + r], part, ident[0:r, 0:r])
                last.then_inc(full, 1)
            pe.wait_ge(in_w_ready, 1)
            for t in range(NT):
                b, r = bank_for("l3_z", t), rows_of(t)
                pe.wait_ge(done["l3_xT"], t + 1)
                for m in range(KT):
                    last = mm(b[0:r, m * P:(m + 1) * P], T2[:, m, t * P:t * P + r], in_w[:, 0 if m == 0 else 1, :], start=True, stop=True)
                last.then_inc(full, 1)

            bF, bU, bW = bank[0], bank[1], (bank[2], bank[3])

            def attrs_T(i, s):
                gi = 2 * i + s
                pe.wait_ge(rec_in[s], 16 * (i + 1))
                if not (isinstance(i, int) and gi == 0):
                    pe.wait_ge(fT_ready, gi)
                for c in range(GROUP):
                    last = nc.tensor.transpose(bF[0:SRC_COLS, c * P:(c + 1) * P], recg[:, s, c, :], ident[:, :])
                last.then_inc(fT_done, 1)

            def filter_in(i, s):
                gi = 2 * i + s
                pe.wait_ge(fT_ready, gi + 1)
                if not (isinstance(i, int) and gi == 0):
                    pe.wait_ge(h_ready, gi)
                mm(bU, wf1_sb, fT[:, s, :], start=True, stop=True).then_inc(u_done, 1)

            def filter_out(i, s, c):
                n = GROUP * (2 * i + s) + c
                if c == 0:
                    pe.wait_ge(h_ready, 2 * i + s + 1)
                if not (isinstance(n, int) and n < 2):
                    pe.wait_ge(msg_ready, n - 1)
                mm(bW[c % 2], hT[:, s, c * P:(c + 1) * P], wf2_sb, start=True, stop=False)
                mm(bW[c % 2], onesb[0:3, :], bf2_b, start=False, stop=True).then_inc(filt_done, 1)

            def scatter(i, s, c):
                gi = 2 * i + s
                n = GROUP * gi + c
                pe.wait_ge(msg_ready, n + 1)
                pe.wait_ge(cmul_ready, n + 1)
                pe.wait_ge(oh_ready, n + 1)
                if c == 0 and not (isinstance(i, int) and gi == 0):
                    pe.wait_ge(agg_added, gi)
                for h in range(2):
                    last = mm(bank[6 + h], oh[:, c, :], msg[:, c, h * D:(h + 1) * D], start=c == 0, stop=c == GROUP - 1)
                last.then_inc(scat_chunk, 1)

            def group(i, s, head=False, tail=False):
                filter_out(i, s, 0)
                if not head:
                    scatter(i if s == 1 else i - 1, 1 - s, GROUP - 1)
                if not tail:
                    attrs_T(i if s == 0 else i + 1, 1 - s)
                filter_out(i, s, 1)
                scatter(i, s, 0)
                filter_out(i, s, 2)
                if not tail:
                    filter_in(i if s == 0 else i + 1, 1 - s)
                scatter(i, s, 1)
                filter_out(i, s, 3)
                scatter(i, s, 2)

            pe.wait_ge(done["l3_z"], NT)
            pe.wait_ge(l3w_ready, 2)
            attrs_T(0, 0)
            filter_in(0, 0)
            group(0, 0, head=True)
            group(0, 1)
            with pe.Fori(1, L3_IT - 1) as i:
                group(i, 0)
                group(i, 1)
            group(L3_IT - 1, 0)
            group(L3_IT - 1, 1, tail=True)
            scatter(L3_IT - 1, 1, GROUP - 1)

            pe.wait_ge(agg_added, GROUPS)
            for t in range(NT):
                s, r = t % 2, rows_of(t)
                if t:
                    pe.wait_ge(aT_ready, 2 * t)
                for m in range(8):
                    col = t * MSG + m * P
                    last = nc.tensor.transpose(bank[m // 4][:, (m % 4) * P:(m % 4) * P + P], agg[:, col:col + P], ident[:, :])
                last.then_inc(t_done, 1)
                pe.wait_ge(aT_ready, 2 * (t + 1))
                if t:
                    pe.wait_ge(svT_ready, t)
                for k in range(2):
                    mm(bank[2][:, 0:P], w1s[:, k, :], aT[:, s, k, :], start=k == 0, stop=k == 1)
                for k in range(2):
                    last = mm(bank[2][:, P:D], w1v[:, k, :], aT[:, s, 2 + 3 * k:5 + 3 * k, :].rearrange("p m n -> p (m n)"),
                              start=k == 0, stop=k == 1)
                last.then_inc(sv_done, 1)
                pe.wait_ge(svT_ready, t + 1)
                if t:
                    pe.wait_ge(o_read, t)
                for m in range(KT):
                    last = mm(bank[3][:, m * P:(m + 1) * P], svT[:, s, m * P:(m + 1) * P], w2sv[:, 0 if m == 0 else 1, :], start=True, stop=True)
                last.then_inc(o_done, 1)

        @block.scalar
        def _(act):
            A = nc.scalar.activation
            link = Chain(act, achain)
            act.dma_start(weight_f, edge_weight.rearrange("(p j) -> p j", p=EP)).then_inc(weight_in, 16)
            for h in range(2):
                act.wait_ge(attr_in, 16 * (h + 1))
                A(rec0[:, h * (EJ // 2):(h + 1) * (EJ // 2), 0:20], attr_half, ACT.Copy).then_inc(attr_used, 1)
            act.wait_ge(attr_used, 2)
            act.wait_ge(weight_in, 16)
            A(rec0[:, :, C_R:C_R + 1], weight_f.unsqueeze(2), ACT.Copy).then_inc(recs_ready, 1)

            act.wait_ge(sq_ready, 1)
            A(tmp_f, tmp_f, ACT.Sqrt).then_inc(norm_ready, 1)

            def sel_w(i):
                for c in range(AB):
                    n = i * AB + c
                    act.wait_ge(sel_ready, n + 1)
                    A(sel_d[:, c, 1, :], sel_d[:, c, 0, :], ACT.Copy,
                      scale=shared[:, ds(n * PAIR_COLS + 2, 1)]).then_inc(selw_ready, 1)

            sel_w(0)
            with act.Fori(1, AB_IT) as i:
                sel_w(i)

            def taken(name, k):
                act.wait_ge(full, first[name] + k + 1)
                return bank[(first[name] + k) % NB]

            for m in range(KT):
                for q, (c0, w) in enumerate(PIECES):
                    A(T1[:, m, c0:c0 + w], taken("l0_agg", m * 3 + q)[:, 0:w], ACT.Copy).then_inc(done["l0_agg"], 1)
            act.wait_ge(b1_in, 16)
            for m in range(KT):
                for q, (c0, w) in enumerate(PIECES):
                    A(T2[:, m, c0:c0 + w], taken("l0_up", m * 3 + q)[:, 0:w], ACT.Relu, bias=b1col[:, m:m + 1]).then_inc(done["l0_up"], 1)

            def copies_T(name):
                for t in range(NT):
                    r = rows_of(t)
                    A(T2[:, :, t * P:t * P + r], taken(name, t).rearrange("p (k n) -> p k n", k=KT)[:, :, 0:r], ACT.Copy).then_inc(done[name], 1)

            def roots(a):
                for t in range(NT):
                    r = rows_of(t)
                    act.wait_ge(var_ready, a * NT + t + 1)
                    A(lnt[0:r, 8:9], lnt[0:r, 8:9], ACT.Sqrt).then_inc(std_ready, 1)

            roots(0)
            copies_T("l1_xT")
            copies_T("l1b_xT")
            roots(1)
            copies_T("l2_xT")
            for t in range(NT):
                r = rows_of(t)
                A(xb[0:r, t, :], taken("l2_h", t)[0:r, :], ACT.Copy).then_inc(done["l2_h"], 1)
            roots(2)
            copies_T("l3_xT")
            for t in range(NT):
                r = rows_of(t)
                A(xb[0:r, t, :], taken("l3_z", t)[0:r, :], ACT.Copy).then_inc(done["l3_z"], 1)
                act.wait_ge(done["l3_z"], t + 1)
                act.dma_start(z_table[t * P:t * P + r, :], xb[0:r, t, :]).then_inc(z_out, 16)

            def attrs(i, s):
                gi = 2 * i + s
                act.wait_ge(fT_done, gi + 1)
                if not (isinstance(gi, int) and gi < 2):
                    act.wait_ge(u_done, gi - 1)
                A(fT[:, s, :], bank[0][0:SRC_COLS, :], ACT.Copy).then_inc(fT_ready, 1)

            def softplus(i, s):
                gi = 2 * i + s
                act.wait_ge(u_done, gi + 1)
                if not (isinstance(gi, int) and gi == 0):
                    act.wait_ge(h_ready, gi)
                A(sp, bank[1], ACT.Abs).then_inc(sp_chain, 1)
                act.wait_ge(sp_chain, 2 * gi + 1)
                A(sp, sp, ACT.Exp, scale=-1.0).then_inc(sp_chain, 1)
                act.wait_ge(sp_chain, 2 * gi + 2)
                A(sp, sp, ACT.Ln, scale=0.5, bias=half_t).then_inc(sp_ready, 1)

            def c_part(i, s, c):
                n = GROUP * (2 * i + s) + c
                act.wait_ge(msg_a, n + 1)
                if not (isinstance(n, int) and n < GROUP):
                    act.wait_ge(scat_chunk, n - GROUP + 1)
                for k in range(3):
                    last = A(msg[:, c, (2 + k) * P:(3 + k) * P], msg[:, c, MSG:MSG + P], ACT.Copy,
                             scale=recg[:, s, c, C_Y + k:C_Y + k + 1])
                last.then_inc(cmul_ready, 1)

            def group(i, s, tail=False):
                nxt = (i, 1) if s == 0 else (i + 1, 0)
                c_part(i, s, 0)
                if not tail:
                    attrs(*nxt)
                c_part(i, s, 1)
                c_part(i, s, 2)
                if not tail:
                    softplus(*nxt)
                c_part(i, s, 3)

            act.wait_ge(l3w_ready, 2)
            attrs(0, 0)
            softplus(0, 0)
            group(0, 0)
            group(0, 1)
            with act.Fori(1, L3_IT - 1) as i:
                group(i, 0)
                group(i, 1)
            group(L3_IT - 1, 0)
            group(L3_IT - 1, 1, tail=True)

            for t in range(NT):
                s, r = t % 2, rows_of(t)
                act.wait_ge(t_done, t + 1)
                if t >= 2:
                    act.wait_ge(sv_done, t - 1)
                for h in range(2):
                    A(aT[:, s, 4 * h:4 * h + 4, :].rearrange("p m n -> p (m n)"), bank[h], ACT.Copy).then_inc(aT_ready, 1)
                act.wait_ge(sv_done, t + 1)
                if t:
                    act.wait_ge(svT_ready, t)
                if t >= 2:
                    act.wait_ge(o_done, t - 1)
                A(svT[:, s, P:D], bank[2][:, P:D], ACT.Copy).then_inc(act_sv, 1)
                link(A(sp[:, 0:P], bank[2][:, 0:P], ACT.Abs))
                link(A(sp[:, 0:P], sp[:, 0:P], ACT.Exp, scale=-1.0))
                A(sp[:, 0:P], sp[:, 0:P], ACT.Ln, scale=0.5, bias=half_t).then_inc(act_sv, 1)
            act.wait_ge(var_ready, 3 * NT + 1)
            A(stat[:, 1, :], stat[:, 1, :], ACT.Sqrt).then_inc(std_ready, 1)
            for t in range(NT):
                act.wait_ge(y_ready, t + 1)
                act.dma_start(out[t * P:t * P + rows_of(t), :], xa[0:rows_of(t), t, :]).then_inc(out_done, 16)
            act.wait_ge(out_done, 16 * NT)

        @block.vector
        def _(dve):
            v = nc.vector
            link = Chain(dve, chain)
            dve.wait_ge(edges_in, 32)
            for a, tile_f, slot in ((src_i, src_tile, 0), (dst_i, dst_tile, 1)):
                link(v.tensor_scalar(tmp_i, a, 7, None, ALU.arith_shift_right))
                link(v.tensor_copy(tile_f, tmp_i))
                if slot == 0:
                    link(v.tensor_scalar(tmp_i, a, P - 1, None, ALU.bitwise_and))
                    link(v.tensor_copy(pair_rec[:, :, 0:1], tmp_i.unsqueeze(2)))
                    link(v.tensor_copy(rec0[:, :, C_SRC:C_SRC + 1], tmp_i.unsqueeze(2)))
                else:
                    link(v.tensor_scalar(tmp_i, a, P - 1, None, ALU.bitwise_and))
                    link(v.tensor_copy(pair_rec[:, :, 1:2], tmp_i.unsqueeze(2)))
                    link(v.tensor_copy(rec0[:, :, C_DST:C_DST + 1], a.unsqueeze(2)))
            link(v.scalar_tensor_tensor(keys[0], src_tile, float(NT), dst_tile, ALU.mult, ALU.add))
            dve.wait_ge(consts, 6)

            def sort(s):
                B, L, q = BUCKETS[s], LOTS_PER_BANK[s], QUANT_LOG2[s]
                W = LT * B
                for t in range(LT):
                    j = slice(t * LJ, (t + 1) * LJ)
                    v.tensor_tensor(ind[s][:, j, :], keys[s][:, j].unsqueeze(2).to_broadcast([EP, LJ, B]),
                                    iota[0:EP, 0:B].unsqueeze(1).to_broadcast([EP, LJ, B]), ALU.is_equal).then_inc(ind_ready[s], 1)
                if s == 0:
                    dve.wait_ge(weight_in, 16)
                    v.tensor_copy(pair_rec[:, :, 2:3], weight_f.unsqueeze(2)).then_inc(pair_rec_ready, 1)
                    v.memset(pair_rec[:, :, 3:4], 0.0).then_inc(pair_rec_ready, 1)
                link(v.memset(step_w[:, 0:B], float(P if s == 0 else MSG)))
                if s == 0:
                    link(v.memset(step_w[:, NT - 1:B:NT], float(N - (NT - 1) * P)))
                link(v.memset(step_w[:, B - 1:B], 0.0))
                dve.wait_ge(cnt_done[s], 1)
                v.tensor_copy(cnt_sb[0:LJ, 0:W], bank[0][0:LJ, 0:W]).then_inc(cnt_sb_ready[s], 1)
                dve.wait_ge(base_done[s], 1)
                link(v.tensor_scalar(nch_i[:, 0:B], bank[2][:, 0:B], float((1 << q) - 1), None, ALU.add))
                link(v.tensor_scalar(nch_i[:, 0:B], nch_i[:, 0:B], q, None, ALU.arith_shift_right))
                link(v.tensor_copy(nch_f[:, 0:B], nch_i[:, 0:B]))
                link(v.tensor_tensor_scan(end_c[:, 0:B], ones_f[:, 0:B], nch_f[:, 0:B], 0.0, ALU.mult, ALU.add))
                link(v.tensor_tensor(start_c[:, 0:B], end_c[:, 0:B], nch_f[:, 0:B], ALU.subtract))
                link(v.tensor_scalar(start_c[:, 0:B], start_c[:, 0:B], float(1 << q), None, ALU.mult))
                view = lambda a: a[0:LJ, 0:W].rearrange("p (t b) -> p t b", b=B)
                link(v.tensor_tensor(view(base_i), view(bank[1]), start_c[0:LJ, 0:B].unsqueeze(1).to_broadcast([LJ, LT, B]), ALU.add))
                link(v.tensor_scalar(base_f[0:LJ, 0:W].bitcast(i32), base_i[0:LJ, 0:W], 255, None, ALU.bitwise_and))
                link(v.tensor_copy(base_lo[0:LJ, 0:W], base_f[0:LJ, 0:W].bitcast(i32)))
                link(v.tensor_tensor(base_i[0:LJ, 0:W], base_i[0:LJ, 0:W], base_f[0:LJ, 0:W].bitcast(i32), ALU.subtract))
                v.tensor_copy(base_hi[0:LJ, 0:W], base_i[0:LJ, 0:W]).then_inc(base_ready[s], 1)
                tiles = math.ceil((PAIR_CHUNKS, GROUPS)[s] / P)
                for t in range(tiles):
                    link(v.tensor_scalar(cmp_w[:, 0:B], end_c[:, 0:B], chunk_no[:, t:t + 1], None, ALU.is_le))
                    link(v.tensor_tensor(cmp_w[:, 0:B], cmp_w[:, 0:B], step_w[:, 0:B], ALU.mult))
                    v.tensor_reduce(offcol[:, t:t + 1], cmp_w[:, 0:B], AX.X, ALU.add).then_inc(offs_ready[s], 1)
                    dve.wait_ge(offs_ready[s], t + 1)
                def select(i, u):
                    n = 2 * i + u
                    dve.wait_ge(pos_done[s], n + 1)
                    if not (isinstance(i, int) and i == 0):
                        dve.wait_ge(pos_step[s], 2 * (n - 1))
                    w = L * B
                    pv = prod[u][:, 0:w]
                    v.tensor_tensor(pv, bank[4 + u][0:EP, 0:w],
                                    ind[s][:, ds(n * L, L), :].rearrange("p a b -> p (a b)"), ALU.mult).then_inc(pos_read[s], 1)
                    dve.wait_ge(pos_read[s], n + 1)
                    v.tensor_reduce(pos_f[:, ds(n * L, L)], pv.rearrange("p (a b) -> p a b", b=B), AX.X, ALU.add).then_inc(pos_step[s], 2)
                for u in range(2):
                    select(0, u)
                with dve.Fori(1, EJ // L // 2) as i:
                    for u in range(2):
                        select(i, u)
                dve.wait_ge(pos_step[s], 2 * (EJ // L))
                link(v.tensor_copy(tmp_i, pos_f))
                link(v.tensor_scalar(tmp2_i, tmp_i, P - 1, None, ALU.bitwise_and))
                link(v.tensor_scalar(tmp_i, tmp_i, 7, None, ALU.arith_shift_right))
                v.scalar_tensor_tensor(rows_i[s][0:EP, :], tmp2_i, float(CHUNKS[s]), tmp_i, ALU.mult, ALU.add).then_inc(rows_ready[s], 1)
                dve.wait_ge(off_done[s], 1)
                n = (PAIR_CHUNKS, P)[s]
                link(v.tensor_copy(offs[s][:, 0:n], bank[3][0:1, 0:n]))

            v.memset(ones_f[:, :], 1.0).then_inc(ones_ready, 1)
            dve.wait_ge(ones_ready, 1)
            sort(0)
            dve.wait_ge(xyz_in, 16)
            sq = ind[0][:, 0:2 * 3 * EJ // BUCKETS[0] + 1, :].rearrange("p a b -> p (a b)")[:, 0:2 * 3 * EJ].bitcast(f32).rearrange("p (j i) -> p j i", i=3)
            link(v.tensor_tensor(sq, xyz, xyz, ALU.mult))
            v.tensor_reduce(tmp_f, sq, AX.X, ALU.add).then_inc(sq_ready, 1)
            dve.wait_ge(norm_ready, 1)
            link(v.reciprocal(tmp_f, tmp_f))
            link(v.tensor_scalar(tmp_f, tmp_f, Y1_SCALE, None, ALU.mult))
            v.tensor_tensor(rec0[:, :, C_Y:C_Y + 3], xyz, tmp_f.unsqueeze(2).to_broadcast([EP, EJ, 3]), ALU.mult).then_inc(recs_ready, 1)
            sort(1)
            v.memset(adj_t[:, :], 0.0).then_inc(offs_read, 1)
            dve.wait_ge(offs_read, 1)

            dve.wait_ge(pair_in, 16)
            dve.wait_ge(rec_out, 16)

            def blocks(i):
                for c in range(AB):
                    n = i * AB + c
                    v.tensor_scalar(sel_s[:, c, :], iota[:, :], shared[:, ds(n * PAIR_COLS, 1)], None, ALU.is_equal)
                    v.tensor_scalar(sel_d[:, c, 0, :], iota[:, :], shared[:, ds(n * PAIR_COLS + 1, 1)], None, ALU.is_equal).then_inc(sel_ready, 1)

            def add(i):
                for c in range(AB):
                    n = i * AB + c
                    off = dve.value_load(offs[0][0:1, ds(n, 1)], min_val=0, max_val=AW_COLS - P)
                    dve.wait_ge(blk_done, n + 1)
                    if not (isinstance(i, int) and n == 0):
                        dve.wait_ge(blk_added, n)
                    a = adj[:, :, ds(off, P)]
                    v.tensor_tensor(a, a, bank[c][:, 0:2 * P].rearrange("p (k n) -> p k n", k=2), ALU.add).then_inc(blk_added, 1)

            blocks(0)
            with dve.Fori(1, AB_IT) as i:
                add(i - 1)
                blocks(i)
            add(AB_IT - 1)

            def taken(name, k):
                dve.wait_ge(full, first[name] + k + 1)
                return bank[(first[name] + k) % NB]

            norms = [0]

            def normalise(y, o, r):
                norms[0] += 1
                link(v.bn_stats(lnt[0:r, 0:6], y))
                link(v.bn_aggr(lnt[0:r, 6:8], lnt[0:r, 0:6]))
                v.tensor_scalar(lnt[0:r, 8:9], lnt[0:r, 7:8], EPS, None, ALU.add).then_inc(var_ready, 1)
                dve.wait_ge(std_ready, norms[0])
                link(v.reciprocal(lnt[0:r, 8:9], lnt[0:r, 8:9]))
                return v.tensor_scalar(o, y, lnt[0:r, 6:7], lnt[0:r, 8:9], ALU.subtract, ALU.mult)

            def residual(name, loaded, relu):
                dve.wait_ge(bias_in, loaded)
                for t in range(NT):
                    r = rows_of(t)
                    y = ybuf[0:r, :]
                    if t:
                        dve.wait_ge(done[name], t)
                    link(v.tensor_tensor(y, taken(name, t)[0:r, :], bias_sb[0:r, :], ALU.add))
                    if relu:
                        link(v.scalar_tensor_tensor(y, y, 0.0, xa[0:r, t, :], ALU.max, ALU.add))
                    else:
                        link(v.tensor_tensor(y, y, xa[0:r, t, :], ALU.add))
                    normalise(y, xa[0:r, t, :], r).then_inc(done[name], 1)

            def scaled_T(name):
                for m in range(KT):
                    for q, (c0, w) in enumerate(PIECES):
                        v.tensor_tensor(T1[:, m, c0:c0 + w], taken(name, m * 3 + q)[:, 0:w], rdeg[:, c0:c0 + w], ALU.mult).then_inc(done[name], 1)

            residual("l0_down", 16, relu=False)
            for q, (c0, w) in enumerate(PIECES):
                link(v.tensor_scalar(rdeg[:, c0:c0 + w], taken("deg", q)[:, 0:w], 1.0, None, ALU.max))
                v.reciprocal(rdeg[:, c0:c0 + w], rdeg[:, c0:c0 + w]).then_inc(done["deg"], 1)
            dve.wait_ge(done["deg"], 3)
            scaled_T("l1a_agg")
            dve.wait_ge(bias_in, 32)
            link(v.memset(xb[:, NT - 1, :], 0.0))
            for t in range(NT):
                r = rows_of(t)
                link(v.tensor_tensor(ybuf[0:r, :], taken("l1a_out", t)[0:r, :], bias_sb[0:r, :], ALU.add))
                v.tensor_scalar(xb[0:r, t, :], ybuf[0:r, :], 0.0, None, ALU.max).then_inc(done["l1a_out"], 1)
                dve.wait_ge(done["l1a_out"], t + 1)
            scaled_T("l1b_agg")
            residual("l1b_out", 48, relu=True)
            residual("l2_agg", 64, relu=True)

            dve.wait_ge(full, first["l2_h"] + NT)
            link(v.memset(wf1_sb, 0.0))
            v.memset(half_t, 0.5).then_inc(l3w_ready, 1)
            dve.wait_ge(l3w_in, 16 * 10)
            v.tensor_scalar(in_w, in_w, P ** -0.5, None, ALU.mult).then_inc(in_w_ready, 1)
            c = (2 * P) ** -0.5
            link(v.tensor_scalar(w1s[:, 0, :], w1s[:, 0, :], c * Y0, None, ALU.mult))
            link(v.tensor_scalar(w1s[:, 1, :], w1s[:, 1, :], c * 3 ** -0.5, None, ALU.mult))
            link(v.tensor_scalar(w1v[:, 0, :], w1v[:, 0, :], c, None, ALU.mult))
            link(v.tensor_scalar(w1v[:, 1, :], w1v[:, 1, :], c * Y0, None, ALU.mult))
            link(v.tensor_scalar(w2sv, w2sv, P ** -0.5, None, ALU.mult))
            def deinterleave(o, i):
                o = o.rearrange("p (k h f) -> p h f k", k=2, h=2)
                i = i.rearrange("p (h f k) -> p h f k", h=2, k=2)
                for h in range(2):
                    link(v.tensor_copy(o[:, h], i[:, h]))
            deinterleave(wf2_sb, wf2_raw)
            deinterleave(bf2_f, bf2_t)
            link(v.memset(bf2_b, 0.0))
            for k in range(3):
                link(v.tensor_copy(bf2_p, bf2_f))
                if k < 2:
                    link(v.tensor_tensor(bf2_f, bf2_f, bf2_p, ALU.subtract))
                link(v.scalar_tensor_tensor(bf2_b, bf2_p, ident[0:3, k:k + 1], bf2_b, ALU.mult, ALU.add))
            v.memset(agg, 0.0).then_inc(l3w_ready, 1)
            dve.wait_ge(l3w_ready, 2)

            def hidden(i, s):
                gi = 2 * i + s
                dve.wait_ge(sp_ready, gi + 1)
                if not (isinstance(gi, int) and gi < 2):
                    dve.wait_ge(filt_done, GROUP * (gi - 1))
                v.scalar_tensor_tensor(hT[:, s, :], bank[1], 0.0, sp, ALU.max, ALU.add).then_inc(h_ready, 1)

            def one_hot(i, s, c):
                n = GROUP * (2 * i + s) + c
                if c == 0:
                    dve.wait_ge(rec_in[s], 16 * (i + 1))
                if not (isinstance(n, int) and n < GROUP):
                    dve.wait_ge(scat_chunk, n - GROUP + 1)
                v.tensor_scalar(oh[:, c, :], iota[:, :], recg[:, s, c, C_SRC:C_SRC + 1], recg[:, s, c, C_R:C_R + 1],
                                ALU.is_equal, ALU.mult).then_inc(oh_ready, 1)

            def messages(i, s, c):
                n = GROUP * (2 * i + s) + c
                b = bank[2 + c % 2]
                dve.wait_ge(filt_done, n + 1)
                dve.wait_ge(z_in[c], 16 * (2 * i + s + 1))
                if not (isinstance(n, int) and n < GROUP):
                    dve.wait_ge(cmul_ready, n - GROUP + 1)
                both = msg[:, c, 0:MSG + P].rearrange("p (a n) -> p a n", n=P)[:, 0:9:8, :]
                v.tensor_tensor(both, zg[:, s, c, 0:P].unsqueeze(1).to_broadcast([P, 2, P]),
                                b[:, 0:2 * P].rearrange("p (a n) -> p a n", a=2), ALU.mult).then_inc(msg_a, 1)
                v.tensor_tensor(msg[:, c, 5 * P:8 * P].rearrange("p (a n) -> p a n", a=3),
                                zg[:, s, c, P:4 * P].rearrange("p (a n) -> p a n", a=3),
                                b[:, 3 * P:4 * P].unsqueeze(1).to_broadcast([P, 3, P]), ALU.mult)
                dve.wait_ge(vy_ready, n + 1)
                v.tensor_tensor(msg[:, c, P:2 * P], vy[:, c, :], b[:, 2 * P:3 * P], ALU.mult).then_inc(msg_ready, 1)

            def add_sums(i, s):
                gi = 2 * i + s
                off = dve.value_load(offs[1][0:1, ds(gi, 1)], min_val=0, max_val=(NT - 1) * MSG)
                dve.wait_ge(scat_chunk, GROUP * (gi + 1))
                if not (isinstance(gi, int) and gi == 0):
                    dve.wait_ge(agg_added, gi)
                a = agg[:, ds(off, MSG)]
                v.tensor_tensor(a, a, ps67[:, :], ALU.add).then_inc(agg_added, 1)

            def group(i, s, head=False, tail=False):
                one_hot(i, s, 0)
                messages(i, s, 0)
                if not head:
                    add_sums(i if s == 1 else i - 1, 1 - s)
                for c in range(1, GROUP):
                    one_hot(i, s, c)
                    messages(i, s, c)
                if not tail:
                    hidden(i if s == 0 else i + 1, 1 - s)

            hidden(0, 0)
            group(0, 0, head=True)
            group(0, 1)
            with dve.Fori(1, L3_IT - 1) as i:
                group(i, 0)
                group(i, 1)
            group(L3_IT - 1, 0)
            group(L3_IT - 1, 1, tail=True)
            add_sums(L3_IT - 1, 1)

            link(v.memset(stat, 1.0))
            for t in range(NT):
                s, r = t % 2, rows_of(t)
                dve.wait_ge(act_sv, 2 * t + 2)
                v.scalar_tensor_tensor(svT[:, s, 0:P], bank[2][:, 0:P], 0.0, sp[:, 0:P], ALU.max, ALU.add).then_inc(svT_ready, 1)
                dve.wait_ge(o_done, t + 1)
                y = xa[0:r, t, :]
                link(v.tensor_tensor(y[:, 0:P], bank[3][0:r, 0:P], y[:, 0:P], ALU.add))
                yv = y[:, P:D].rearrange("p (d i) -> p i d", i=3)
                v.tensor_tensor(yv, bank[3][0:r, P:D].rearrange("p (i d) -> p i d", i=3), yv, ALU.add).then_inc(o_read, 1)
                dve.wait_ge(o_read, t + 1)
                link(v.bn_stats(lnt[0:r, 0:6], y))
                link(v.bn_aggr(stat[0:r, :, t], lnt[0:r, 0:6]))
            v.tensor_scalar(stat[:, 1, :], stat[:, 1, :], EPS, None, ALU.add).then_inc(var_ready, 1)
            dve.wait_ge(std_ready, 3 * NT + 1)
            link(v.reciprocal(stat[:, 1, :], stat[:, 1, :]))
            for t in range(NT):
                y = xa[0:rows_of(t), t, :]
                r = rows_of(t)
                v.tensor_scalar(y, y, stat[0:r, 0, t:t + 1], stat[0:r, 1, t:t + 1], ALU.subtract, ALU.mult).then_inc(y_ready, 1)


def kernel(x, src, dst, edge_attr_20, edge_attr_3, edge_weight, L0_gnn_W1, L0_gnn_b1, L0_gnn_W2, L0_gnn_b2,
           L1_gnn_W_self1, L1_gnn_W_neigh1, L1_gnn_b1, L1_gnn_W_self2, L1_gnn_W_neigh2, L1_gnn_b2,
           L2_gnn_W, L2_gnn_bias, L3_gnn_W_in2f_s, L3_gnn_W_in2f_v, L3_gnn_Wf1, L3_gnn_bf1, L3_gnn_Wf2, L3_gnn_bf2,
           L3_gnn_W1_s, L3_gnn_W1_v, L3_gnn_W2_s, L3_gnn_W2_v):
    import concourse.bacc as _bacc
    from concourse.bass_utils import run_bass_kernel_spmd as _run

    given = dict(x=x, src=src, dst=dst, edge_attr_20=edge_attr_20, edge_attr_3=edge_attr_3, edge_weight=edge_weight,
                 l0_w1=L0_gnn_W1, l0_b1=L0_gnn_b1, l0_w2=L0_gnn_W2, l0_b2=L0_gnn_b2,
                 l1_ws1=L1_gnn_W_self1, l1_wn1=L1_gnn_W_neigh1, l1_b1=L1_gnn_b1,
                 l1_ws2=L1_gnn_W_self2, l1_wn2=L1_gnn_W_neigh2, l1_b2=L1_gnn_b2,
                 l2_w=L2_gnn_W, l2_b=L2_gnn_bias, w_in_s=L3_gnn_W_in2f_s, w_in_v=L3_gnn_W_in2f_v,
                 wf1=L3_gnn_Wf1, bf1=L3_gnn_bf1, wf2=L3_gnn_Wf2, bf2=L3_gnn_bf2,
                 w1_s=L3_gnn_W1_s, w1_v=L3_gnn_W1_v, w2_s=L3_gnn_W2_s, w2_v=L3_gnn_W2_v)
    nc = _bacc.Bacc("TRN2", target_bir_lowering=False, num_devices=1)
    arrays, aps = {}, {}
    for name, a in given.items():
        a = np.ascontiguousarray(a)
        arrays["in_" + name] = a
        aps[name] = nc.dram_tensor("in_" + name, a.shape, mybir.dt.from_np(a.dtype), kind="ExternalInput").ap()
    aps["out"] = nc.dram_tensor("out_x", (N, D), mybir.dt.float32, kind="ExternalOutput").ap()
    build(nc, **aps)
    r = _run(nc, [arrays], core_ids=[0])
    return r.results[0]["out_x"]
```

```python
import math
from contextlib import ExitStack

import numpy as np
import concourse.bass as bass
from concourse import mybir

P = 128
N, D, E = 1250, 512, 40000
NT = (N + P - 1) // P
TAIL = N - (NT - 1) * P
KT = D // P
PIECES = [(0, 512), (512, 512), (1024, N - 1024)]

EP, EJ = 125, 320
LT = 5
LJ = EJ // LT

BUCKETS = [NT * NT, NT]
QUANT_LOG2 = [7, 9]
LOTS_PER_BANK = [4, 32]
AB = 4
PAIR_CHUNKS = 2 * AB * math.ceil((E + BUCKETS[0] * (P - 1)) // P / (2 * AB))
GROUP = 4
GROUPS = (E + NT * (GROUP * P - 1)) // (GROUP * P)
GROUPS += GROUPS % 2
SRC_CHUNKS = GROUPS * GROUP
CHUNKS = [PAIR_CHUNKS, SRC_CHUNKS]
PAIR_COLS, SRC_COLS = 4, 32
STAGED = [8, 4]

FILL = 44
RELEASES = [2, 1]
assert SRC_CHUNKS % FILL == 0

C_ONE, C_Y, C_R, C_SRC, C_DST = 20, 21, 24, 25, 26
ATT = 21
SIDE = C_DST - ATT
PRODUCTS = 6

AW_COLS = (NT - 1) * N + NT * P
MSG = 8 * P

Y0 = float(1.0 / np.sqrt(4.0 * np.pi))
Y1_SCALE = float(np.sqrt(3.0 / (4.0 * np.pi)))
EPS = 1e-5

STAGES = [("l0_xT", NT), ("l0_up", NT), ("l0_agg", 12), ("l0_down", NT),
          ("l1_xT", NT), ("deg", 3), ("l1a_agg", 12), ("l1a_out", NT),
          ("l1b_xT", NT), ("l1b_agg", 12), ("l1b_out", NT),
          ("l2_xT", NT), ("l2_h", NT), ("l2_agg", NT), ("l3_xT", NT), ("l3_z", NT)]
NB = 8


def build(nc, x, src, dst, edge_attr_20, edge_attr_3, edge_weight,
          l0_w1, l0_b1, l0_w2, l0_b2, l1_ws1, l1_wn1, l1_b1, l1_ws2, l1_wn2, l1_b2,
          l2_w, l2_b, w_in_s, w_in_v, wf1, bf1, wf2, bf2, w1_s, w1_v, w2_s, w2_v, out):
    f32, bf16, i32, u32 = mybir.dt.float32, mybir.dt.bfloat16, mybir.dt.int32, mybir.dt.uint32
    ALU, ACT, AX = mybir.AluOpType, mybir.ActivationFunctionType, mybir.AxisListType
    ds = bass.ds

    tables = [nc.dram_tensor("pair_table", [P * PAIR_CHUNKS, PAIR_COLS], f32, kind="Internal").ap(),
              nc.dram_tensor("src_table", [P * SRC_CHUNKS, SRC_COLS], f32, kind="Internal").ap()]
    records = nc.dram_tensor("records", [EP, EJ * SRC_COLS], f32, kind="Internal").ap()
    z_table = nc.dram_tensor("z_table", [N, D], f32, kind="Internal").ap()

    ctx = ExitStack()
    with ctx:
        def sb(name, shape, dt=f32):
            return ctx.enter_context(nc.sbuf_tensor(name, shape, dt))

        def sem(name):
            return ctx.enter_context(nc.semaphore(name))

        adj_t = sb("adj_t", [P, 2 * AW_COLS])
        adj = adj_t[:, :].rearrange("p (k n) -> p k n", k=2)
        dense = sb("dense", [P, NT * D + 2 * KT * N])
        xb = dense[:, 0:NT * D].rearrange("p (t n) -> p t n", t=NT)
        T1 = dense[:, NT * D:NT * D + KT * N].rearrange("p (k n) -> p k n", k=KT)
        T2 = dense[:, NT * D + KT * N:NT * D + 2 * KT * N].rearrange("p (k n) -> p k n", k=KT)
        xa_t = sb("xa", [P, NT * D])
        xa = xa_t[:, :].rearrange("p (t n) -> p t n", t=NT)
        wring = sb("wring", [P, 2, KT, D])
        shared = sb("shared", [P, N + D])
        pair_sb = shared[:, 0:PAIR_CHUNKS * PAIR_COLS].rearrange("p (c w) -> p c w", w=PAIR_COLS)
        rdeg = shared[:, 0:N]
        bias_sb = shared[:, N:N + D]
        iota = sb("iota", [P, P])
        ident = sb("ident", [P, P])
        onesb = sb("onesb", [P, P], bf16)
        trib = sb("trib", [P, P], bf16)
        tri2 = sb("tri2", [LJ, P], bf16)
        ident2 = sb("ident2", [P, LJ], bf16)
        iotab = sb("iotab", [P, P], bf16)
        window = sb("window", [P, 2 * LJ], bf16)
        ones_f = sb("ones_f", [P, P])
        pcol = sb("pcol", [P, 1])
        ybuf = sb("ybuf", [P, D])
        rows_i = [dense[:, 14592:14592 + EJ].bitcast(i32), sb("src_rows", [P, EJ], i32)[:, :]]
        offs = [ybuf[0:1, 0:PAIR_CHUNKS].bitcast(i32), sb("src_offs", [1, P], i32)[:, :]]
        b1col = sb("b1col", [P, KT])
        lnt = sb("lnt", [P, 12])

        at = [0]

        def carve(parts, n, dt=f32):
            words = n if dt != bf16 else (n + 1) // 2
            v = adj_t[0:parts, at[0]:at[0] + words]
            at[0] += words
            return v if dt == f32 else v.bitcast(dt)

        ind = [carve(EP, EJ * b, bf16).rearrange("p (j b) -> p j b", b=b) for b in BUCKETS]
        src_i, dst_i, tmp_i, tmp2_i = [carve(EP, EJ, i32) for _ in range(4)]
        src_tile, dst_tile, tmp_f, weight_f = [carve(EP, EJ) for _ in range(4)]
        keys = [carve(EP, EJ), src_tile]
        pos_f = carve(EP, EJ)
        xyz = carve(EP, 3 * EJ).rearrange("p (j i) -> p j i", i=3)
        prod_w = max(LOTS_PER_BANK[s] * BUCKETS[s] for s in range(2))
        prod = [carve(EP, prod_w) for _ in range(2)]
        zeros_w = carve(P, LT * BUCKETS[0], bf16)
        cnt_sb = carve(P, LT * BUCKETS[0], bf16)
        rest_i = carve(P, LT * BUCKETS[0], i32)
        base_i = carve(P, LT * BUCKETS[0], i32)
        base_parts = carve(P, LT * BUCKETS[0], bf16)
        nch_i, end_c, start_c, step_w, cmp_w, nch_f = [carve(P, BUCKETS[0], i32 if k == 0 else f32) for k in range(6)]
        offcol = carve(P, 4)
        chunk_no = carve(P, 4)
        fill = dense[:, 12928:12928 + PAIR_CHUNKS * PAIR_COLS]
        assert at[0] <= 2 * AW_COLS
        rec0 = dense[0:EP, 0:EJ * SRC_COLS].rearrange("p (j w) -> p j w", w=SRC_COLS)
        pair_rec = dense[0:EP, EJ * SRC_COLS:EJ * (SRC_COLS + PAIR_COLS)].rearrange("p (j w) -> p j w", w=PAIR_COLS)
        attr_half = wring[0:EP, :, :, :].rearrange("p a b c -> p (a b c)")[:, 0:EJ // 2 * 20].rearrange("p (j w) -> p j w", w=20)
        fill32 = dense[:, EJ * (SRC_COLS + PAIR_COLS):EJ * (SRC_COLS + PAIR_COLS) + FILL * SRC_COLS].rearrange("p (c w) -> p c w", w=SRC_COLS)

        st_idx = sb("st_idx", [P, 2, max(STAGED)], i32)
        st_rec = sb("st_rec", [P, 2, 4 * SRC_COLS])

        sel_b = dense[:, 0:2 * AB * P].bitcast(bf16).rearrange("p (c k n) -> p c k n", k=2, n=P)
        sel_f = dense[:, 2 * AB * P:6 * AB * P].rearrange("p (c k n) -> p c k n", k=2, n=P)

        xT0 = adj_t[:, 4000:4000 + KT * N].rearrange("p (k n) -> p k n", k=KT)

        at[0] = 0
        agg = carve(P, NT * MSG)
        zg = carve(P, 2 * GROUP * D).rearrange("p (s c n) -> p s c n", s=2, c=GROUP)
        recg = carve(P, 2 * GROUP * SRC_COLS).rearrange("p (s c w) -> p s c w", s=2, c=GROUP)
        side = carve(P, 2 * GROUP * SIDE).rearrange("p (s c w) -> p s c w", s=2, c=GROUP)
        dsti = carve(P, 2 * GROUP, i32).rearrange("p (s c) -> p s c", s=2)
        msg = carve(P, GROUP * (MSG + P)).rearrange("p (c n) -> p c n", c=GROUP)
        hT = carve(P, 2 * D).rearrange("p (s n) -> p s n", s=2)
        att = carve(P, 2 * GROUP * PRODUCTS * ATT, bf16).rearrange("p (s c k w) -> p s c k w", s=2, c=GROUP, k=PRODUCTS)
        att_rest = carve(P, GROUP * ATT).rearrange("p (c w) -> p c w", c=GROUP)
        fT = carve(PRODUCTS * ATT, 2 * D, bf16).rearrange("p (s n) -> p s n", s=2)
        identb = carve(P, P, bf16)
        sp = carve(P, D)
        vy = carve(P, GROUP * P).rearrange("p (c n) -> p c n", c=GROUP)
        oh = carve(P, GROUP * P).rearrange("p (c n) -> p c n", c=GROUP)
        aT = carve(P, 2 * MSG).rearrange("p (s m n) -> p s m n", s=2, m=8)
        svT = T1[:, 1, 0:2 * D].rearrange("p (s n) -> p s n", s=2)
        assert at[0] <= 2 * AW_COLS
        wl = wring[:, :, :, :].rearrange("p a b c -> p (a b c)")
        wl_at = [0]

        def wcarve(parts, n, dt=f32):
            words = n if dt != bf16 else n // 2
            v = wl[0:parts, wl_at[0]:wl_at[0] + words]
            wl_at[0] += words
            return v if dt == f32 else v.bitcast(dt)

        in_w = wcarve(P, 2 * P).rearrange("p (k n) -> p k n", k=2)
        w1s = wcarve(P, 2 * P).rearrange("p (k n) -> p k n", k=2)
        w1v = wcarve(P, 2 * P).rearrange("p (k n) -> p k n", k=2)
        w2sv = wcarve(P, 2 * P).rearrange("p (k n) -> p k n", k=2)
        wf1_f = wcarve(PRODUCTS * ATT, P)
        wf1_h = wcarve(PRODUCTS * ATT, P, bf16)
        wf1_sb = wcarve(PRODUCTS * ATT, P, bf16)
        part_w = wcarve(PRODUCTS * ATT, 4)
        wf2_sb = wcarve(P, D)
        bf2_f = wcarve(3, D)
        bf2_t = wcarve(3, D)
        bf2_b = wcarve(3, D, bf16)
        bf2_p = wcarve(3, D, bf16)
        half_t = wcarve(P, 1)
        stat = ybuf[:, 0:2 * NT].rearrange("p (k t) -> p k t", k=2)
        wf2_raw = T1[:, 0, 0:D]

        ps = [ctx.enter_context(nc.psum_tensor(f"ps{i}", [P, 512], f32)) for i in range(6)]
        ps67 = ctx.enter_context(nc.psum_tensor("ps67", [P, 1024], f32))
        bank = [ps[i][:, :] for i in range(6)] + [ps67[:, 0:512], ps67[:, 512:1024]]

        fT_bank = bank[0].bitcast(bf16)[0:PRODUCTS * ATT, 0:D]

        edges_in, weight_in, xyz_in, x_in = sem("edges_in"), sem("weight_in"), sem("xyz_in"), sem("x_in")
        attr_in, attr_used = sem("attr_in"), sem("attr_used")
        consts = sem("consts")
        filled, rec_out = sem("filled"), sem("rec_out")
        fill_ready = sem("fill_ready")
        recs_ready = sem("recs_ready")
        ind_ready = [sem(f"ind_ready{s}") for s in range(2)]
        cnt_done = [sem(f"cnt_done{s}") for s in range(2)]
        cnt_sb_ready = [sem(f"cnt_sb_ready{s}") for s in range(2)]
        base_done = [sem(f"base_done{s}") for s in range(2)]
        base_ready = [sem(f"base_ready{s}") for s in range(2)]
        pos_done = [sem(f"pos_done{s}") for s in range(2)]
        pos_read = [sem(f"pos_read{s}") for s in range(2)]
        off_done = [sem(f"off_done{s}") for s in range(2)]
        rows_ready = [sem(f"rows_ready{s}") for s in range(2)]
        offs_ready = [sem(f"offs_ready{s}") for s in range(2)]
        tick = sem("tick")
        chain = sem("chain")
        gchain = sem("gchain")
        achain = sem("achain")
        staged = [sem(f"staged{s}") for s in range(2)]
        scat = [[sem(f"scat{s}{k}") for k in range(2)] for s in range(2)]
        st_load = [sem(f"st_load{k}") for k in range(2)]
        pair_in = sem("pair_in")
        sq_ready, norm_ready = sem("sq_ready"), sem("norm_ready")
        var_ready, std_ready = sem("var_ready"), sem("std_ready")
        pair_rec_ready = sem("pair_rec_ready")
        ones_ready = sem("ones_ready")
        pos_step = [sem(f"pos_step{s}") for s in range(2)]
        offs_out, adj_zero = sem("offs_out"), sem("adj_zero")
        x_again = sem("x_again")
        sel_ready = sem("sel_ready")
        selw_ready = sem("selw_ready")
        blk_done, blk_added = sem("blk_done"), sem("blk_added")
        full = sem("full")
        done = {name: sem("done_" + name) for name, _ in STAGES}
        w_in = [sem(f"w_in{k}") for k in range(2)]
        bias_in, b1_in = sem("bias_in"), sem("b1_in")
        z_out = sem("z_out")
        l3w_in, l3w_ready = sem("l3w_in"), sem("l3w_ready")
        in_w_ready = sem("in_w_ready")
        rec_in = [sem(f"rec_in{k}") for k in range(2)]
        z_in = [[sem(f"z_in{s}{c}") for c in range(GROUP)] for s in range(2)]
        dsti_ready, att_step, side_ready = sem("dsti_ready"), sem("att_step"), sem("side_ready")
        fT_done, fT_ready, u_done, sp_ready, h_ready = sem("fT_done"), sem("fT_ready"), sem("u_done"), sem("sp_ready"), sem("h_ready")
        sp_chain = sem("sp_chain")
        vy_chain = sem("vy_chain")
        oh_ready = sem("oh_ready")
        filt_done, msg_a, msg_ready, cmul_ready = sem("filt_done"), sem("msg_a"), sem("msg_ready"), sem("cmul_ready")
        scat_chunk = sem("scat_chunk")
        agg_added = sem("agg_added")
        agg_zero = sem("agg_zero")
        t_done, aT_ready, sv_done, svT_ready, o_done, o_read = sem("t_done"), sem("aT_ready"), sem("sv_done"), sem("svT_ready"), sem("o_done"), sem("o_read")
        act_sv = sem("act_sv")
        y_ready, out_done = sem("y_ready"), sem("out_done")

        def wait_alone(eng, s, value):
            eng.wait_ge(s, value).then_inc(tick, 1)

        class Chain:
            def __init__(self, eng, s):
                self.eng, self.s, self.n = eng, s, 0

            def __call__(self, ins):
                self.n += 1
                ins.then_inc(self.s, 1)
                self.eng.wait_ge(self.s, self.n)

        first = {}
        total = 0
        for name, count in STAGES:
            first[name] = total
            total += count
        place = [(name, k) for name, count in STAGES for k in range(count)]

        def rows_of(t):
            return P if t < NT - 1 else TAIL

        SCATTERED = 16 * EJ // 2
        AB_IT = PAIR_CHUNKS // (2 * AB)
        L3_IT = GROUPS // 2
        L3_LOADS = 8 + 2 * PRODUCTS

        block = ctx.enter_context(nc.Block())

        @block.sync
        def _(sp_eng):
            sp_eng.dma_start(src_i, src.rearrange("(p j) -> p j", p=EP)).then_inc(edges_in, 16)
            sp_eng.dma_start(dst_i, dst.rearrange("(p j) -> p j", p=EP)).then_inc(edges_in, 16)
            sp_eng.wait_ge(fill_ready, 2)
            sp_eng.dma_start(tables[0].rearrange("(p c) w -> p (c w)", p=P), fill).then_inc(filled, 16)
            t1 = tables[1].rearrange("(p c) w -> p c w", p=P)
            for c in range(0, SRC_CHUNKS, FILL):
                sp_eng.dma_start(t1[:, c:c + FILL, :], fill32).then_inc(filled, 16)
            sp_eng.dma_start(xyz, edge_attr_3.rearrange("(p j) i -> p j i", p=EP)).then_inc(xyz_in, 16)
            attr = edge_attr_20.rearrange("(p j) w -> p j w", p=EP)
            for h in range(2):
                if h:
                    sp_eng.wait_ge(attr_used, h)
                sp_eng.dma_start(attr_half, attr[:, h * (EJ // 2):(h + 1) * (EJ // 2), :]).then_inc(attr_in, 16)
            sp_eng.wait_ge(x_in, 1)
            sp_eng.dma_start(xa[:, 0:NT - 1, :], x[0:(NT - 1) * P, :].rearrange("(t p) n -> p t n", p=P)).then_inc(x_in, 16)
            sp_eng.dma_start(xa[0:TAIL, NT - 1, :], x[(NT - 1) * P:N, :]).then_inc(x_in, 16)
            sp_eng.wait_ge(recs_ready, 3)
            sp_eng.dma_start(records, rec0.rearrange("p j w -> p (j w)")).then_inc(rec_out, 16)
            sp_eng.dma_start(b1col[:, :], l0_b1.rearrange("(m p) -> p m", p=P), allow_slow_non_contiguous=True).then_inc(b1_in, 16)
            ring = [(l0_w1, None), (l0_w2, None), (l1_ws1, "l0_agg"), (l1_wn1, "l0_down"),
                    (l1_ws2, "l1a_out"), (l1_wn2, "l1a_out"), (l2_w, "l1b_out")]
            sp_eng.wait_ge(attr_used, 2)
            biases = {1: (l0_b2, None), 3: (l1_b1, "l0_down"), 5: (l1_b2, "l1a_out"), 6: (l2_b, "l1b_out")}
            for q, (w, after) in enumerate(ring):
                if after:
                    sp_eng.wait_ge(full, first[after] + dict(STAGES)[after])
                sp_eng.dma_start(wring[:, q % 2, :, :], w.rearrange("(t k) n -> k t n", k=P)).then_inc(w_in[q % 2], 16)
                if q == 1:
                    for k in range(2):
                        sp_eng.wait_ge(scat[0][k], SCATTERED)
                    sp_eng.dma_start(pair_sb.rearrange("p c w -> p (c w)"),
                                     tables[0].rearrange("(p c) w -> p (c w)", p=P)).then_inc(pair_in, 16)
                    sp_eng.wait_ge(blk_added, PAIR_CHUNKS)
                    sp_eng.dma_start(xb[:, 0:NT - 1, :], x[0:(NT - 1) * P, :].rearrange("(t p) n -> p t n", p=P)).then_inc(x_again, 16)
                    sp_eng.dma_start(xb[0:TAIL, NT - 1, :], x[(NT - 1) * P:N, :]).then_inc(x_again, 16)
                if q in biases:
                    b, after = biases[q]
                    if after:
                        sp_eng.wait_ge(done[after], NT)
                    sp_eng.dma_start(bias_sb, b.partition_broadcast(P)).then_inc(bias_in, 16)
            sp_eng.wait_ge(full, first["l2_h"] + NT)
            loads = [(in_w[:, 0, :], w_in_s), (in_w[:, 1, :], w_in_v),
                     (w1s, w1_s.rearrange("(f k) c -> f k c", k=2)), (w1v, w1_v.rearrange("(f k) c -> f k c", k=2)),
                     (w2sv[:, 0, :], w2_s), (w2sv[:, 1, :], w2_v), (bf2_t, bf2[0:D].partition_broadcast(3)),
                     (wf2_raw, wf2[:, 0:D])]
            for k in range(PRODUCTS):
                loads += [(wf1_f[k * ATT:(k + 1) * ATT - 1, :], wf1), (wf1_f[(k + 1) * ATT - 1:(k + 1) * ATT, :], bf1.rearrange("(a n) -> a n", a=1))]
            assert len(loads) == L3_LOADS
            for o, i in loads:
                sp_eng.dma_start(o, i).then_inc(l3w_in, 16)

            tsrc = tables[1].rearrange("(p c) w -> p (c w)", p=P)

            def load_group(i, s):
                g = 2 * i + s
                if not isinstance(i, int) or i > 0:
                    wait_alone(sp_eng, att_step, 4 * (g - 1))
                    wait_alone(sp_eng, side_ready, g - 1)
                    wait_alone(sp_eng, dsti_ready, g - 1)
                sp_eng.dma_start(recg[:, s, :, :].rearrange("p c w -> p (c w)"),
                                 tsrc[:, ds(g * (GROUP * SRC_COLS), GROUP * SRC_COLS)]).then_inc(rec_in[s], 16)

            for k in range(2):
                sp_eng.wait_ge(scat[1][k], SCATTERED)
            sp_eng.wait_ge(full, first["l2_agg"] + NT)
            load_group(0, 0)
            load_group(0, 1)
            with sp_eng.Fori(1, L3_IT) as i:
                load_group(i, 0)
                load_group(i, 1)

        @block.gpsimd
        def _(pool):
            g = nc.gpsimd
            link = Chain(pool, gchain)
            link(g.memset(window[:, :], 0.0))
            link(g.memset(window[:, LJ - 1:LJ], 1.0))
            link(g.memset(onesb[:, :], 1.0))
            link(g.memset(zeros_w, 0.0))
            link(g.iota(iota[:, :], [[1, P]], base=0, channel_multiplier=0, allow_small_or_imprecise_dtypes=True))
            link(g.iota(pcol[:, :], [[0, 1]], base=0, channel_multiplier=1, allow_small_or_imprecise_dtypes=True))
            link(g.iota(chunk_no, [[P, 4]], base=0, channel_multiplier=1, allow_small_or_imprecise_dtypes=True))
            link(g.tensor_scalar(ident[:, :], iota[:, :], pcol[:, :], None, ALU.is_equal))
            link(g.tensor_scalar(trib[:, :], iota[:, :], pcol[:, :], None, ALU.is_gt))
            for h in range(2):
                link(g.tensor_scalar(tri2[:, h * LJ:(h + 1) * LJ], iota[0:LJ, 0:LJ], pcol[0:LJ, :], None, ALU.is_gt))
                link(g.tensor_copy(ident2[h * LJ:(h + 1) * LJ, :], ident[h * LJ:(h + 1) * LJ, h * LJ:(h + 1) * LJ]))
            g.tensor_copy(iotab[:, :], iota[:, :]).then_inc(consts, 1)
            link(g.memset(fill, 0.0))
            fv = fill.rearrange("p (c w) -> p c w", w=PAIR_COLS)
            g.memset(fv[:, :, 0:2], -1.0).then_inc(fill_ready, 1)
            link(g.memset(fill32, 0.0))
            g.memset(fill32[:, :, C_SRC:C_SRC + 1], -1.0).then_inc(fill_ready, 1)
            g.memset(xa[:, NT - 1, :], 0.0).then_inc(x_in, 1)
            link(g.memset(rec0[:, :, C_DST + 1:SRC_COLS], 0.0))
            g.memset(rec0[:, :, C_ONE:C_ONE + 1], 1.0).then_inc(recs_ready, 1)

            def stage(s, t, i, k):
                n = STAGED[s]
                j = i * (2 * n) + (t * LJ + k * n)
                if s == 0:
                    g.tensor_copy(st_rec[0:EP, k, 0:n * PAIR_COLS],
                                  dense[0:EP, ds(j * PAIR_COLS + EJ * SRC_COLS, n * PAIR_COLS)]).then_inc(staged[s], 1)
                else:
                    pool.dma_start(st_rec[0:EP, k, :], records[:, ds(j * SRC_COLS, n * SRC_COLS)]).then_inc(st_load[k], 16)
                g.tensor_copy(st_idx[0:EP, k, 0:n], rows_i[s][0:EP, ds(j, n)]).then_inc(staged[s], 1)

            def scatter(s, m, k):
                n, w = STAGED[s], (PAIR_COLS, SRC_COLS)[s]
                per = (2, 1)[s]
                wait_alone(pool, staged[s], per * (2 * m + k + 1))
                if s == 1:
                    wait_alone(pool, st_load[k], 16 * (m + 1))
                for c in range(n):
                    g.indirect_dma_start(out=tables[s], out_offset=bass.IndirectOffsetOnAxis(ap=st_idx[0:EP, k, c:c + 1].bitcast(u32), axis=0),
                                         in_=st_rec[0:EP, k, c * w:(c + 1) * w], in_offset=None).then_inc(scat[s][k], 16)

            for s in range(2):
                turns = LJ // (2 * STAGED[s])

                def turn(t, i):
                    m = i + t * turns
                    for k in range(2):
                        if not isinstance(m, int) or m > 0:
                            wait_alone(pool, scat[s][k], 16 * STAGED[s] * m)
                        stage(s, t, i, k)
                        scatter(s, m, k)

                for t, q in [(t, q) for t in range(LT) for q in range(RELEASES[s])]:
                    pool.wait_ge(rows_ready[s], t * RELEASES[s] + q + 1)
                    start = q * turns // RELEASES[s]
                    if t == 0 and q == 0:
                        start = 1
                        if s == 0:
                            pool.wait_ge(pair_rec_ready, 2)
                            pool.wait_ge(filled, 16 * (1 + SRC_CHUNKS // FILL))
                        else:
                            pool.wait_ge(rec_out, 16)
                            for k in range(2):
                                pool.wait_ge(scat[0][k], SCATTERED)
                        turn(0, 0)
                    with pool.Fori(start, (q + 1) * turns // RELEASES[s]) as i:
                        turn(t, i)

            def split(i, s):
                gi = 2 * i + s
                if not (isinstance(gi, int) and gi < 2):
                    wait_alone(pool, fT_done, gi - 1)
                x, parts = recg[:, s, :, 0:ATT], att[:, s, :, :, :]
                g.tensor_copy(parts[:, :, 0:3, :], x.unsqueeze(2).to_broadcast([P, GROUP, 3, ATT])).then_inc(att_step, 1)
                wait_alone(pool, att_step, 4 * gi + 1)
                g.tensor_tensor(att_rest, x, parts[:, :, 0, :], ALU.subtract).then_inc(att_step, 1)
                wait_alone(pool, att_step, 4 * gi + 2)
                g.tensor_copy(parts[:, :, 3:5, :], att_rest.unsqueeze(2).to_broadcast([P, GROUP, 2, ATT])).then_inc(att_step, 1)
                wait_alone(pool, att_step, 4 * gi + 3)
                g.tensor_tensor(parts[:, :, 5, :], att_rest, parts[:, :, 3, :], ALU.subtract).then_inc(att_step, 1)

            def gather(i, s, c):
                gi = 2 * i + s
                n = GROUP * gi + c
                if c == 0:
                    wait_alone(pool, rec_in[s], 16 * (i + 1))
                    split(i, s)
                    if not (isinstance(gi, int) and gi < 2):
                        wait_alone(pool, msg_ready, GROUP * (gi - 1))
                        wait_alone(pool, cmul_ready, GROUP * (gi - 1))
                    g.tensor_copy(side[:, s, :, :], recg[:, s, :, ATT:ATT + SIDE]).then_inc(side_ready, 1)
                    g.tensor_copy(dsti[:, s, :], recg[:, s, :, C_DST]).then_inc(dsti_ready, 1)
                    wait_alone(pool, dsti_ready, gi + 1)
                    if isinstance(gi, int) and gi == 0:
                        pool.wait_ge(z_out, 16 * NT)
                if not (isinstance(n, int) and n < 2 * GROUP):
                    wait_alone(pool, msg_ready, n - 2 * GROUP + 1)
                g.indirect_dma_start(out=zg[:, s, c, :], out_offset=None, in_=z_table,
                                     in_offset=bass.IndirectOffsetOnAxis(ap=dsti[:, s, c:c + 1].bitcast(u32), axis=0)).then_inc(z_in[s][c], 16)

            def group(i, s, tail=False):
                nxt = (i, 1) if s == 0 else (i + 1, 0)
                for c in range(GROUP):
                    if c < 2:
                        gather(i, s, c + 2)
                    elif not tail:
                        gather(*nxt, c - 2)

            pool.wait_ge(full, first["l2_agg"] + NT)
            g.memset(agg, 0.0).then_inc(agg_zero, 1)
            gather(0, 0, 0)
            gather(0, 0, 1)
            group(0, 0)
            group(0, 1)
            with pool.Fori(1, L3_IT - 1) as i:
                group(i, 0)
                group(i, 1)
            group(L3_IT - 1, 0)
            group(L3_IT - 1, 1, tail=True)

        @block.tensor
        def _(pe):
            mm = nc.tensor.matmul
            def bank_for(name, k):
                n = first[name] + k
                if n >= NB:
                    before, kb = place[n - NB]
                    pe.wait_ge(done[before], kb + 1)
                return bank[n % NB]

            def agg_T(name, feats, ready, k_of):
                for m in range(KT):
                    for q, (c0, w) in enumerate(PIECES):
                        b = bank_for(name, m * 3 + q)
                        for t in range(NT):
                            if m == 0 and q == 0 and ready is not None:
                                pe.wait_ge(ready, t + 1)
                            last = mm(b[:, 0:w], feats[:, t, m * P:(m + 1) * P], adj[:, k_of, t * N + c0:t * N + c0 + w],
                                      start=t == 0, stop=t == NT - 1 and name != "l0_agg")
                        if name == "l0_agg":
                            tiles = [t for t in range(NT) if c0 <= t * P < c0 + w]
                            for t in tiles:
                                r = rows_of(t)
                                last = mm(b[:, t * P - c0:t * P - c0 + r], feats[:, t, m * P:(m + 1) * P], ident[:, 0:r],
                                          start=False, stop=t == tiles[-1])
                        last.then_inc(full, 1)

            def transposed(name, feats, ready):
                for t in range(NT):
                    b, r = bank_for(name, t), rows_of(t)
                    if ready is not None:
                        pe.wait_ge(ready, t + 1)
                    for m in range(KT):
                        last = nc.tensor.transpose(b[:, m * P:m * P + r], feats[0:r, t, m * P:(m + 1) * P], ident[0:r, 0:r])
                    last.then_inc(full, 1)

            def rows_product(name, parts):
                for t in range(NT):
                    b, r = bank_for(name, t), rows_of(t)
                    for a, (lhs, w) in enumerate(parts):
                        for k in range(KT):
                            last = mm(b[0:r, :], lhs[:, k, t * P:t * P + r], w[:, k, :], start=a == 0 and k == 0,
                                      stop=a == len(parts) - 1 and k == KT - 1)
                    last.then_inc(full, 1)

            pe.wait_ge(consts, 1)
            for s in range(2):
                B, L = BUCKETS[s], LOTS_PER_BANK[s]
                W = LT * B
                mm(bank[0][0:LJ, 0:W], zeros_w[0:EP, 0:LJ], zeros_w[0:EP, 0:W], start=True, stop=False)
                for t in range(LT):
                    pe.wait_ge(ind_ready[s], t + 1)
                    if s == 0:
                        for j in range(LJ):
                            mm(bank[0][0:LJ, t * B:(t + 1) * B], window[0:EP, LJ - 1 - j:2 * LJ - 1 - j],
                               ind[s][:, t * LJ + j, :], start=False, stop=False)
                    else:
                        with pe.Fori(0, LJ // 8) as i:
                            for u in range(8):
                                mm(bank[0][0:LJ, t * B:(t + 1) * B], window[0:EP, ds(LJ - 1 - u - i * 8, LJ)],
                                   ind[s][:, ds(i * 8 + (t * LJ + u), 1), :].rearrange("p a b -> p (a b)"), start=False, stop=False)
                mm(bank[0][0:LJ, 0:W], zeros_w[0:EP, 0:LJ], zeros_w[0:EP, 0:W], start=False, stop=True).then_inc(cnt_done[s], 1)
                pe.wait_ge(cnt_sb_ready[s], 1)
                for t in range(LT):
                    for t2 in range(t + 1):
                        lhs = tri2[:, :] if t2 == t else onesb[0:LJ, :]
                        mm(bank[1][:, t * B:(t + 1) * B], lhs, cnt_sb[0:LJ, t2 * B:(t2 + 1) * B],
                           start=t2 == 0, stop=t2 == t)
                for t in range(LT):
                    last = mm(bank[2][:, 0:B], onesb[0:LJ, :], cnt_sb[0:LJ, t * B:(t + 1) * B], start=t == 0, stop=t == LT - 1)
                last.then_inc(base_done[s], 1)
                pe.wait_ge(base_ready[s], 2)
                nb = LJ // L

                def ranks(t, i, u):
                    b = 4 + u
                    n = i * 2 + (t * nb + u)
                    if not (isinstance(n, int) and n < 2):
                        pe.wait_ge(pos_read[s], n - 1)
                    j = (i * 2 + u) * L
                    mm(bank[b][0:EP, 0:L * B], trib[0:EP, 0:EP],
                       ind[s][:, ds(j + t * LJ, L), :].rearrange("p a b -> p (a b)"), start=True, stop=False)
                    for c in range(L):
                        col = ident2[:, ds(j + c, 1)].to_broadcast([P, EP])
                        last = mm(bank[b][0:EP, c * B:(c + 1) * B], col, base_parts[:, t * B:(t + 1) * B], start=False, stop=c == L - 1)
                    last.then_inc(pos_done[s], 1)

                for t in range(LT):
                    if t == 0:
                        for u in range(2):
                            ranks(0, 0, u)
                    if nb > 2 or t > 0:
                        with pe.Fori(1 if t == 0 else 0, nb // 2) as i:
                            for u in range(2):
                                ranks(t, i, u)
                tiles = math.ceil((PAIR_CHUNKS, GROUPS)[s] / P)
                pe.wait_ge(offs_ready[s], tiles)
                for t in range(tiles):
                    last = mm(bank[3][0:1, t * P:(t + 1) * P], offcol[:, t:t + 1], ident[:, :], start=True, stop=True)
                last.then_inc(off_done[s], 1)

            def blocks(i, h):
                for c in range(h * AB, (h + 1) * AB):
                    n = i * (2 * AB) + c
                    if c == h * AB and not (isinstance(i, int) and i == 0):
                        pe.wait_ge(blk_added, n - AB)
                    pe.wait_ge(selw_ready, n + 1)
                    mm(bank[c][:, 0:P], sel_b[:, c, 0, :], sel_b[:, c, 1, :], start=True, stop=True)
                    mm(bank[c][:, P:2 * P], sel_f[:, c, 0, :], sel_f[:, c, 1, :], start=True, stop=True).then_inc(blk_done, 1)

            def x_times_w1():
                pe.wait_ge(x_in, 33)
                transposed("l0_xT", xa, None)
                pe.wait_ge(w_in[0], 16)
                pe.wait_ge(done["l0_xT"], NT)
                rows_product("l0_up", [(xT0, wring[:, 0, :, :])])

            w0, w1 = wring[:, 0, :, :], wring[:, 1, :, :]
            pe.wait_ge(offs_out, 2)
            x_times_w1()
            pe.wait_ge(adj_zero, 1)
            pe.wait_ge(done["l0_up"], NT)
            blocks(0, 0)
            blocks(0, 1)
            with pe.Fori(1, AB_IT) as i:
                blocks(i, 0)
                blocks(i, 1)
            pe.wait_ge(blk_added, PAIR_CHUNKS)
            agg_T("l0_agg", xa, None, 0)
            pe.wait_ge(w_in[1], 16)
            pe.wait_ge(done["l0_agg"], 12)
            rows_product("l0_down", [(T2, w1)])
            transposed("l1_xT", xa, done["l0_down"])
            for q, (c0, w) in enumerate(PIECES):
                b = bank_for("deg", q)
                pe.wait_ge(ones_ready, 1)
                for t in range(NT):
                    last = mm(b[:, 0:w], ones_f[:, :], adj[:, 0, t * N + c0:t * N + c0 + w], start=t == 0, stop=t == NT - 1)
                last.then_inc(full, 1)
            agg_T("l1a_agg", xa, None, 0)
            pe.wait_ge(w_in[0], 32)
            pe.wait_ge(w_in[1], 32)
            pe.wait_ge(done["l1_xT"], NT)
            pe.wait_ge(done["l1a_agg"], 12)
            rows_product("l1a_out", [(T2, w0), (T1, w1)])
            transposed("l1b_xT", xb, done["l1a_out"])
            agg_T("l1b_agg", xb, None, 0)
            pe.wait_ge(w_in[0], 48)
            pe.wait_ge(w_in[1], 48)
            pe.wait_ge(done["l1b_xT"], NT)
            pe.wait_ge(done["l1b_agg"], 12)
            rows_product("l1b_out", [(T2, w0), (T1, w1)])
            transposed("l2_xT", xa, done["l1b_out"])
            pe.wait_ge(w_in[0], 64)
            pe.wait_ge(done["l2_xT"], NT)
            rows_product("l2_h", [(T2, w0)])
            pe.wait_ge(done["l2_h"], NT)
            for t in range(NT):
                b, r = bank_for("l2_agg", t), rows_of(t)
                for k in range(NT):
                    last = mm(b[0:r, :], adj[0:rows_of(k), 1, k * N + t * P:k * N + t * P + r], xb[0:rows_of(k), k, :],
                              start=k == 0, stop=k == NT - 1)
                last.then_inc(full, 1)
            for t in range(NT):
                b, r = bank_for("l3_xT", t), rows_of(t)
                pe.wait_ge(done["l2_agg"], t + 1)
                for m in range(KT):
                    part = xa[0:r, t, 0:P] if m == 0 else xa[0:r, t, P + m - 1:D:3]
                    last = nc.tensor.transpose(b[:, m * P:m * P + r], part, ident[0:r, 0:r])
                last.then_inc(full, 1)
            pe.wait_ge(in_w_ready, 1)
            for t in range(NT):
                b, r = bank_for("l3_z", t), rows_of(t)
                pe.wait_ge(done["l3_xT"], t + 1)
                for m in range(KT):
                    last = mm(b[0:r, m * P:(m + 1) * P], T2[:, m, t * P:t * P + r], in_w[:, 0 if m == 0 else 1, :], start=True, stop=True)
                last.then_inc(full, 1)

            bU, bW = bank[1], bank[2:2 + GROUP]

            def attrs_T(i, s):
                gi = 2 * i + s
                pe.wait_ge(att_step, 4 * gi + 4)
                if not (isinstance(i, int) and gi == 0):
                    pe.wait_ge(fT_ready, gi)
                for c in range(GROUP):
                    last = nc.tensor.transpose(fT_bank[:, c * P:(c + 1) * P], att[:, s, c, :, :].rearrange("p k w -> p (k w)"), identb)
                last.then_inc(fT_done, 1)

            def filter_in(i, s):
                gi = 2 * i + s
                pe.wait_ge(fT_ready, gi + 1)
                if not (isinstance(i, int) and gi == 0):
                    pe.wait_ge(h_ready, gi)
                mm(bU, wf1_sb, fT[:, s, :], start=True, stop=True).then_inc(u_done, 1)

            def filter_out(i, s, c):
                n = GROUP * (2 * i + s) + c
                if c == 0:
                    pe.wait_ge(h_ready, 2 * i + s + 1)
                if not (isinstance(n, int) and n < GROUP):
                    pe.wait_ge(msg_ready, n - GROUP + 1)
                mm(bW[c], hT[:, s, c * P:(c + 1) * P], wf2_sb, start=True, stop=False)
                mm(bW[c], onesb[0:3, :], bf2_b, start=False, stop=True).then_inc(filt_done, 1)

            def scatter(i, s, c):
                gi = 2 * i + s
                n = GROUP * gi + c
                pe.wait_ge(msg_ready, n + 1)
                pe.wait_ge(cmul_ready, n + 1)
                pe.wait_ge(oh_ready, n + 1)
                if c == 0 and not (isinstance(i, int) and gi == 0):
                    pe.wait_ge(agg_added, gi)
                for h in range(2):
                    last = mm(bank[6 + h], oh[:, c, :], msg[:, c, h * D:(h + 1) * D], start=c == 0, stop=c == GROUP - 1)
                last.then_inc(scat_chunk, 1)

            def group(i, s, tail=False):
                nxt = (i, 1) if s == 0 else (i + 1, 0)
                filter_out(i, s, 2)
                if not tail:
                    attrs_T(*nxt)
                scatter(i, s, 0)
                if not tail:
                    filter_in(*nxt)
                filter_out(i, s, 3)
                scatter(i, s, 1)
                scatter(i, s, 2)
                if not tail:
                    filter_out(*nxt, 0)
                scatter(i, s, 3)
                if not tail:
                    filter_out(*nxt, 1)

            pe.wait_ge(done["l3_z"], NT)
            pe.wait_ge(l3w_ready, 2)
            attrs_T(0, 0)
            filter_in(0, 0)
            filter_out(0, 0, 0)
            filter_out(0, 0, 1)
            group(0, 0)
            group(0, 1)
            with pe.Fori(1, L3_IT - 1) as i:
                group(i, 0)
                group(i, 1)
            group(L3_IT - 1, 0)
            group(L3_IT - 1, 1, tail=True)

            pe.wait_ge(agg_added, GROUPS)
            tbank = [(bank[0], bank[1]), (bank[4], bank[5])]
            svbank, obank = (bank[2], bank[6]), (bank[3], bank[7])

            def sums_T(t):
                s = t % 2
                if t >= 2:
                    pe.wait_ge(aT_ready, 2 * (t - 1))
                for m in range(8):
                    col = t * MSG + m * P
                    last = nc.tensor.transpose(tbank[s][m // 4][:, (m % 4) * P:(m % 4) * P + P], agg[:, col:col + P], ident[:, :])
                last.then_inc(t_done, 1)

            def mixed(t):
                s = t % 2
                pe.wait_ge(aT_ready, 2 * (t + 1))
                if t >= 2:
                    pe.wait_ge(svT_ready, t - 1)
                for k in range(2):
                    mm(svbank[s][:, 0:P], w1s[:, k, :], aT[:, s, k, :], start=k == 0, stop=k == 1)
                for k in range(2):
                    last = mm(svbank[s][:, P:D], w1v[:, k, :], aT[:, s, 2 + 3 * k:5 + 3 * k, :].rearrange("p m n -> p (m n)"),
                              start=k == 0, stop=k == 1)
                last.then_inc(sv_done, 1)

            def outputs(t):
                s = t % 2
                pe.wait_ge(svT_ready, t + 1)
                if t >= 2:
                    pe.wait_ge(o_read, t - 1)
                for m in range(KT):
                    last = mm(obank[s][:, m * P:(m + 1) * P], svT[:, s, m * P:(m + 1) * P], w2sv[:, 0 if m == 0 else 1, :], start=True, stop=True)
                last.then_inc(o_done, 1)

            sums_T(0)
            for t in range(NT):
                if t + 1 < NT:
                    sums_T(t + 1)
                mixed(t)
                if t:
                    outputs(t - 1)
            outputs(NT - 1)

        @block.scalar
        def _(act):
            A = nc.scalar.activation
            link = Chain(act, achain)
            act.dma_start(weight_f, edge_weight.rearrange("(p j) -> p j", p=EP)).then_inc(weight_in, 16)
            for h in range(2):
                act.wait_ge(attr_in, 16 * (h + 1))
                A(rec0[:, h * (EJ // 2):(h + 1) * (EJ // 2), 0:20], attr_half, ACT.Copy).then_inc(attr_used, 1)
            act.wait_ge(attr_used, 2)
            act.wait_ge(weight_in, 16)
            A(rec0[:, :, C_R:C_R + 1], weight_f.unsqueeze(2), ACT.Copy).then_inc(recs_ready, 1)

            act.wait_ge(sq_ready, 1)
            A(tmp_f, tmp_f, ACT.Sqrt).then_inc(norm_ready, 1)

            def taken(name, k):
                act.wait_ge(full, first[name] + k + 1)
                return bank[(first[name] + k) % NB]

            def copies_T(name, to=T2):
                for t in range(NT):
                    r = rows_of(t)
                    A(to[:, :, t * P:t * P + r], taken(name, t).rearrange("p (k n) -> p k n", k=KT)[:, :, 0:r], ACT.Copy).then_inc(done[name], 1)

            copies_T("l0_xT", xT0)
            for t in range(NT):
                A(xa[0:rows_of(t), t, :], taken("l0_up", t)[0:rows_of(t), :], ACT.Copy).then_inc(done["l0_up"], 1)

            def sel_w(i, h):
                for c in range(h * AB, (h + 1) * AB):
                    n = i * (2 * AB) + c
                    act.wait_ge(sel_ready, n + 1)
                    A(sel_f[:, c, 0, :], sel_b[:, c, 0, :], ACT.Copy)
                    A(sel_f[:, c, 1, :], sel_b[:, c, 1, :], ACT.Copy, scale=shared[:, ds(n * PAIR_COLS + 2, 1)]).then_inc(selw_ready, 1)

            for h in range(2):
                sel_w(0, h)
            with act.Fori(1, AB_IT) as i:
                for h in range(2):
                    sel_w(i, h)

            act.wait_ge(b1_in, 16)
            for m in range(KT):
                for q, (c0, w) in enumerate(PIECES):
                    A(T2[:, m, c0:c0 + w], taken("l0_agg", m * 3 + q)[:, 0:w], ACT.Relu, bias=b1col[:, m:m + 1]).then_inc(done["l0_agg"], 1)

            def roots(a):
                for t in range(NT):
                    r = rows_of(t)
                    act.wait_ge(var_ready, a * NT + t + 1)
                    A(lnt[0:r, 8:9], lnt[0:r, 8:9], ACT.Sqrt).then_inc(std_ready, 1)

            roots(0)
            copies_T("l1_xT")
            copies_T("l1b_xT")
            roots(1)
            copies_T("l2_xT")
            for t in range(NT):
                r = rows_of(t)
                A(xb[0:r, t, :], taken("l2_h", t)[0:r, :], ACT.Copy).then_inc(done["l2_h"], 1)
            roots(2)
            copies_T("l3_xT")
            for t in range(NT):
                r = rows_of(t)
                A(xb[0:r, t, :], taken("l3_z", t)[0:r, :], ACT.Copy).then_inc(done["l3_z"], 1)
                act.wait_ge(done["l3_z"], t + 1)
                act.dma_start(z_table[t * P:t * P + r, :], xb[0:r, t, :]).then_inc(z_out, 16)

            def attrs(i, s):
                gi = 2 * i + s
                act.wait_ge(fT_done, gi + 1)
                if not (isinstance(gi, int) and gi < 2):
                    act.wait_ge(u_done, gi - 1)
                A(fT[:, s, :], fT_bank, ACT.Copy).then_inc(fT_ready, 1)

            def softplus_exp(i, s):
                gi = 2 * i + s
                act.wait_ge(u_done, gi + 1)
                if not (isinstance(gi, int) and gi == 0):
                    act.wait_ge(h_ready, gi)
                A(sp, bank[1], ACT.Abs).then_inc(sp_chain, 1)
                act.wait_ge(sp_chain, 2 * gi + 1)
                A(sp, sp, ACT.Exp, scale=-1.0).then_inc(sp_chain, 1)

            def softplus_log(i, s):
                gi = 2 * i + s
                act.wait_ge(sp_chain, 2 * gi + 2)
                A(sp, sp, ACT.Ln, scale=0.5, bias=half_t).then_inc(sp_ready, 1)

            def c_part(i, s, c):
                n = GROUP * (2 * i + s) + c
                act.wait_ge(msg_a, n + 1)
                if not (isinstance(n, int) and n < GROUP):
                    act.wait_ge(scat_chunk, n - GROUP + 1)
                for k in range(3):
                    last = A(msg[:, c, (2 + k) * P:(3 + k) * P], msg[:, c, MSG:MSG + P], ACT.Copy,
                             scale=side[:, s, c, C_Y - ATT + k:C_Y - ATT + k + 1])
                last.then_inc(cmul_ready, 1)

            def group(i, s, tail=False):
                nxt = (i, 1) if s == 0 else (i + 1, 0)
                c_part(i, s, 0)
                if not tail:
                    attrs(*nxt)
                c_part(i, s, 1)
                if not tail:
                    softplus_exp(*nxt)
                c_part(i, s, 2)
                if not tail:
                    softplus_log(*nxt)
                c_part(i, s, 3)

            act.wait_ge(l3w_ready, 2)
            nc.scalar.preload_act_table_set("natural_log_exp_and_others")
            attrs(0, 0)
            softplus_exp(0, 0)
            softplus_log(0, 0)
            group(0, 0)
            group(0, 1)
            with act.Fori(1, L3_IT - 1) as i:
                group(i, 0)
                group(i, 1)
            group(L3_IT - 1, 0)
            group(L3_IT - 1, 1, tail=True)

            def sums(t):
                s = t % 2
                act.wait_ge(t_done, t + 1)
                if t >= 2:
                    act.wait_ge(sv_done, t - 1)
                for h in range(2):
                    A(aT[:, s, 4 * h:4 * h + 4, :].rearrange("p m n -> p (m n)"), bank[4 * s + h], ACT.Copy).then_inc(aT_ready, 1)

            sums(0)
            for t in range(NT):
                s = t % 2
                if t + 1 < NT:
                    sums(t + 1)
                act.wait_ge(sv_done, t + 1)
                if t >= 2:
                    act.wait_ge(o_done, t - 1)
                    act.wait_ge(svT_ready, t - 1)
                sv = bank[2 + 4 * s]
                A(svT[:, s, P:D], sv[:, P:D], ACT.Copy).then_inc(act_sv, 1)
                spt = sp[:, s * P:(s + 1) * P]
                link(A(spt, sv[:, 0:P], ACT.Abs))
                link(A(spt, spt, ACT.Exp, scale=-1.0))
                A(spt, spt, ACT.Ln, scale=0.5, bias=half_t).then_inc(act_sv, 1)
            act.wait_ge(var_ready, 3 * NT + 1)
            A(stat[:, 1, :], stat[:, 1, :], ACT.Sqrt).then_inc(std_ready, 1)
            for t in range(NT):
                act.wait_ge(y_ready, t + 1)
                act.dma_start(out[t * P:t * P + rows_of(t), :], xa[0:rows_of(t), t, :]).then_inc(out_done, 16)
            act.wait_ge(out_done, 16 * NT)

        @block.vector
        def _(dve):
            v = nc.vector
            link = Chain(dve, chain)
            dve.wait_ge(edges_in, 32)
            for a, tile_f, slot in ((src_i, src_tile, 0), (dst_i, dst_tile, 1)):
                link(v.tensor_scalar(tmp_i, a, 7, None, ALU.arith_shift_right))
                link(v.tensor_copy(tile_f, tmp_i))
                if slot == 0:
                    link(v.tensor_scalar(tmp_i, a, P - 1, None, ALU.bitwise_and))
                    link(v.tensor_copy(pair_rec[:, :, 0:1], tmp_i.unsqueeze(2)))
                    link(v.tensor_copy(rec0[:, :, C_SRC:C_SRC + 1], tmp_i.unsqueeze(2)))
                else:
                    link(v.tensor_scalar(tmp_i, a, P - 1, None, ALU.bitwise_and))
                    link(v.tensor_copy(pair_rec[:, :, 1:2], tmp_i.unsqueeze(2)))
                    link(v.tensor_copy(rec0[:, :, C_DST:C_DST + 1], a.unsqueeze(2)))
            link(v.scalar_tensor_tensor(keys[0], src_tile, float(NT), dst_tile, ALU.mult, ALU.add))
            dve.wait_ge(consts, 1)

            def sort(s):
                B, L, q = BUCKETS[s], LOTS_PER_BANK[s], QUANT_LOG2[s]
                W = LT * B
                for t in range(LT):
                    j = slice(t * LJ, (t + 1) * LJ)
                    v.tensor_tensor(ind[s][:, j, :], keys[s][:, j].unsqueeze(2).to_broadcast([EP, LJ, B]),
                                    iota[0:EP, 0:B].unsqueeze(1).to_broadcast([EP, LJ, B]), ALU.is_equal).then_inc(ind_ready[s], 1)
                if s == 0:
                    dve.wait_ge(weight_in, 16)
                    v.tensor_copy(pair_rec[:, :, 2:3], weight_f.unsqueeze(2)).then_inc(pair_rec_ready, 1)
                    v.memset(pair_rec[:, :, 3:4], 0.0).then_inc(pair_rec_ready, 1)
                link(v.memset(step_w[:, 0:B], float(P if s == 0 else MSG)))
                if s == 0:
                    link(v.memset(step_w[:, NT - 1:B:NT], float(N - (NT - 1) * P)))
                link(v.memset(step_w[:, B - 1:B], 0.0))
                dve.wait_ge(cnt_done[s], 1)
                v.tensor_copy(cnt_sb[0:LJ, 0:W], bank[0][0:LJ, 0:W]).then_inc(cnt_sb_ready[s], 1)
                dve.wait_ge(base_done[s], 1)
                link(v.tensor_scalar(nch_i[:, 0:B], bank[2][:, 0:B], float((1 << q) - 1), None, ALU.add))
                link(v.tensor_scalar(nch_i[:, 0:B], nch_i[:, 0:B], q, None, ALU.arith_shift_right))
                link(v.tensor_copy(nch_f[:, 0:B], nch_i[:, 0:B]))
                link(v.tensor_tensor_scan(end_c[:, 0:B], ones_f[:, 0:B], nch_f[:, 0:B], 0.0, ALU.mult, ALU.add))
                link(v.tensor_tensor(start_c[:, 0:B], end_c[:, 0:B], nch_f[:, 0:B], ALU.subtract))
                link(v.tensor_scalar(start_c[:, 0:B], start_c[:, 0:B], float(1 << q), None, ALU.mult))
                view = lambda a: a[:, 0:W].rearrange("p (t b) -> p t b", b=B)
                link(v.tensor_tensor(view(base_i), view(bank[1]), start_c[:, 0:B].unsqueeze(1).to_broadcast([P, LT, B]), ALU.add))
                link(v.tensor_scalar(rest_i[:, 0:W], base_i[:, 0:W], 255, None, ALU.bitwise_and))
                v.tensor_copy(base_parts[LJ:P, 0:W], rest_i[LJ:P, 0:W]).then_inc(base_ready[s], 1)
                v.tensor_tensor(base_parts[0:LJ, 0:W], base_i[0:LJ, 0:W], rest_i[0:LJ, 0:W], ALU.subtract).then_inc(base_ready[s], 1)
                tiles = math.ceil((PAIR_CHUNKS, GROUPS)[s] / P)
                for t in range(tiles):
                    link(v.tensor_scalar(cmp_w[:, 0:B], end_c[:, 0:B], chunk_no[:, t:t + 1], None, ALU.is_le))
                    link(v.tensor_tensor(cmp_w[:, 0:B], cmp_w[:, 0:B], step_w[:, 0:B], ALU.mult))
                    v.tensor_reduce(offcol[:, t:t + 1], cmp_w[:, 0:B], AX.X, ALU.add).then_inc(offs_ready[s], 1)
                    dve.wait_ge(offs_ready[s], t + 1)
                nb = LJ // L

                def select(t, i, u):
                    n = 2 * i + (t * nb + u)
                    dve.wait_ge(pos_done[s], n + 1)
                    if not (isinstance(n, int) and n < 2):
                        dve.wait_ge(pos_step[s], n - 1)
                    w = L * B
                    pv = prod[u][:, 0:w]
                    v.tensor_tensor(pv, bank[4 + u][0:EP, 0:w],
                                    ind[s][:, ds(n * L, L), :].rearrange("p a b -> p (a b)"), ALU.mult).then_inc(pos_read[s], 1)
                    dve.wait_ge(pos_read[s], n + 1)
                    v.tensor_reduce(pos_f[:, ds(n * L, L)], pv.rearrange("p (a b) -> p a b", b=B), AX.X, ALU.add).then_inc(pos_step[s], 1)

                step, lots = nb // 2 // RELEASES[s], LJ // RELEASES[s]
                for t, q in [(t, q) for t in range(LT) for q in range(RELEASES[s])]:
                    start = q * step
                    if t == 0 and q == 0:
                        start = 1
                        for u in range(2):
                            select(0, 0, u)
                    if start < (q + 1) * step:
                        with dve.Fori(start, (q + 1) * step) as i:
                            for u in range(2):
                                select(t, i, u)
                    dve.wait_ge(pos_step[s], nb * t + 2 * (q + 1) * step)
                    j = slice(t * LJ + q * lots, t * LJ + (q + 1) * lots)
                    link(v.tensor_copy(tmp_i[:, j], pos_f[:, j]))
                    link(v.tensor_scalar(tmp2_i[:, j], tmp_i[:, j], P - 1, None, ALU.bitwise_and))
                    link(v.tensor_scalar(tmp_i[:, j], tmp_i[:, j], 7, None, ALU.arith_shift_right))
                    v.scalar_tensor_tensor(rows_i[s][0:EP, j], tmp2_i[:, j], float(CHUNKS[s]), tmp_i[:, j], ALU.mult, ALU.add).then_inc(rows_ready[s], 1)
                dve.wait_ge(off_done[s], 1)
                n = (PAIR_CHUNKS, P)[s]
                v.tensor_copy(offs[s][:, 0:n], bank[3][0:1, 0:n]).then_inc(offs_out, 1)
                dve.wait_ge(offs_out, s + 1)

            v.memset(ones_f[:, :], 1.0).then_inc(ones_ready, 1)
            dve.wait_ge(ones_ready, 1)
            sort(0)
            dve.wait_ge(xyz_in, 16)
            sq = ind[0][:, 0:2 * 3 * EJ // BUCKETS[0] + 1, :].rearrange("p a b -> p (a b)")[:, 0:2 * 3 * EJ].bitcast(f32).rearrange("p (j i) -> p j i", i=3)
            link(v.tensor_tensor(sq, xyz, xyz, ALU.mult))
            v.tensor_reduce(tmp_f, sq, AX.X, ALU.add).then_inc(sq_ready, 1)
            dve.wait_ge(norm_ready, 1)
            link(v.reciprocal(tmp_f, tmp_f))
            link(v.tensor_scalar(tmp_f, tmp_f, Y1_SCALE, None, ALU.mult))
            v.tensor_tensor(rec0[:, :, C_Y:C_Y + 3], xyz, tmp_f.unsqueeze(2).to_broadcast([EP, EJ, 3]), ALU.mult).then_inc(recs_ready, 1)
            sort(1)
            dve.wait_ge(full, first["l0_up"] + NT)
            v.memset(adj_t[:, :], 0.0).then_inc(adj_zero, 1)
            dve.wait_ge(adj_zero, 1)

            dve.wait_ge(pair_in, 16)
            dve.wait_ge(rec_out, 16)

            def select(i, c):
                n = i * (2 * AB) + c
                col = n * PAIR_COLS
                v.tensor_scalar(sel_b[:, c, 0, :], iotab[:, :], shared[:, ds(col, 1)], None, ALU.is_equal)
                v.tensor_scalar(sel_b[:, c, 1, :], iotab[:, :], shared[:, ds(col + 1, 1)], None, ALU.is_equal).then_inc(sel_ready, 1)

            def half(i, h, first=False, last=False):
                n = i * (2 * AB) + h * AB
                if not last:
                    if not first:
                        dve.wait_ge(blk_done, n - AB)
                    select(i, h * AB)
                if not first:
                    before = n - 2 * AB
                    _, places = nc.values_load_multi_w_load_instructions(
                        offs[0][0:1, ds(before, AB)], engines=[mybir.EngineType.DVE], min_val=0, max_val=AW_COLS - P,
                        skip_runtime_bounds_check_because="a sum of some of the steps between blocks; all of them make the last block's place")
                for k in range(AB):
                    if not first:
                        if last and k == 0:
                            dve.wait_ge(blk_done, before + AB)
                        if not (isinstance(n, int) and before + k == 0):
                            dve.wait_ge(blk_added, before + k)
                        a = adj[:, :, ds(places[k], P)]
                        v.tensor_tensor(a, a, bank[h * AB + k][:, 0:2 * P].rearrange("p (k n) -> p k n", k=2), ALU.add).then_inc(blk_added, 1)
                    if not last and k < AB - 1:
                        select(i, h * AB + k + 1)

            for h in range(2):
                half(0, h, first=True)
            for h in range(2):
                half(1, h)
            with dve.Fori(2, AB_IT) as i:
                for h in range(2):
                    half(i, h)
            for h in range(2):
                half(AB_IT, h, last=True)

            def taken(name, k):
                dve.wait_ge(full, first[name] + k + 1)
                return bank[(first[name] + k) % NB]

            norms = [0]

            def normalise(y, o, r):
                norms[0] += 1
                link(v.bn_stats(lnt[0:r, 0:6], y))
                link(v.bn_aggr(lnt[0:r, 6:8], lnt[0:r, 0:6]))
                v.tensor_scalar(lnt[0:r, 8:9], lnt[0:r, 7:8], EPS, None, ALU.add).then_inc(var_ready, 1)
                dve.wait_ge(std_ready, norms[0])
                link(v.reciprocal(lnt[0:r, 8:9], lnt[0:r, 8:9]))
                return v.tensor_scalar(o, y, lnt[0:r, 6:7], lnt[0:r, 8:9], ALU.subtract, ALU.mult)

            def residual(name, loaded, relu, old=xa):
                dve.wait_ge(bias_in, loaded)
                for t in range(NT):
                    r = rows_of(t)
                    y = ybuf[0:r, :]
                    if t:
                        dve.wait_ge(done[name], t)
                    link(v.tensor_tensor(y, taken(name, t)[0:r, :], bias_sb[0:r, :], ALU.add))
                    if relu:
                        link(v.scalar_tensor_tensor(y, y, 0.0, old[0:r, t, :], ALU.max, ALU.add))
                    else:
                        link(v.tensor_tensor(y, y, old[0:r, t, :], ALU.add))
                    normalise(y, xa[0:r, t, :], r).then_inc(done[name], 1)

            def scaled_T(name):
                for m in range(KT):
                    for q, (c0, w) in enumerate(PIECES):
                        v.tensor_tensor(T1[:, m, c0:c0 + w], taken(name, m * 3 + q)[:, 0:w], rdeg[:, c0:c0 + w], ALU.mult).then_inc(done[name], 1)

            dve.wait_ge(x_again, 32)
            residual("l0_down", 16, relu=False, old=xb)
            for q, (c0, w) in enumerate(PIECES):
                link(v.tensor_scalar(rdeg[:, c0:c0 + w], taken("deg", q)[:, 0:w], 1.0, None, ALU.max))
                v.reciprocal(rdeg[:, c0:c0 + w], rdeg[:, c0:c0 + w]).then_inc(done["deg"], 1)
            dve.wait_ge(done["deg"], 3)
            scaled_T("l1a_agg")
            dve.wait_ge(bias_in, 32)
            link(v.memset(xb[:, NT - 1, :], 0.0))
            for t in range(NT):
                r = rows_of(t)
                link(v.tensor_tensor(ybuf[0:r, :], taken("l1a_out", t)[0:r, :], bias_sb[0:r, :], ALU.add))
                v.tensor_scalar(xb[0:r, t, :], ybuf[0:r, :], 0.0, None, ALU.max).then_inc(done["l1a_out"], 1)
                dve.wait_ge(done["l1a_out"], t + 1)
            scaled_T("l1b_agg")
            residual("l1b_out", 48, relu=True)
            residual("l2_agg", 64, relu=True)

            dve.wait_ge(full, first["l2_h"] + NT)
            v.memset(half_t, 0.5).then_inc(l3w_ready, 1)
            dve.wait_ge(l3w_in, 16 * L3_LOADS)
            v.tensor_scalar(in_w, in_w, P ** -0.5, None, ALU.mult).then_inc(in_w_ready, 1)
            c = (2 * P) ** -0.5
            link(v.tensor_scalar(w1s[:, 0, :], w1s[:, 0, :], c * Y0, None, ALU.mult))
            link(v.tensor_scalar(w1s[:, 1, :], w1s[:, 1, :], c * 3 ** -0.5, None, ALU.mult))
            link(v.tensor_scalar(w1v[:, 0, :], w1v[:, 0, :], c, None, ALU.mult))
            link(v.tensor_scalar(w1v[:, 1, :], w1v[:, 1, :], c * Y0, None, ALU.mult))
            link(v.tensor_scalar(w2sv, w2sv, P ** -0.5, None, ALU.mult))
            def deinterleave(o, i):
                o = o.rearrange("p (k h f) -> p h f k", k=2, h=2)
                i = i.rearrange("p (h f k) -> p h f k", h=2, k=2)
                for h in range(2):
                    link(v.tensor_copy(o[:, h], i[:, h]))
            link(v.tensor_copy(identb, ident[:, :]))
            row = pcol[0:PRODUCTS * ATT, :]
            for k, lo, hi in ((0, ATT, 3 * ATT), (1, 4 * ATT, 5 * ATT), (2, 2 * ATT, 3 * ATT)):
                link(v.tensor_scalar(part_w[:, 3:4], row, float(lo), None, ALU.is_ge))
                link(v.scalar_tensor_tensor(part_w[:, k:k + 1], row, float(hi), part_w[:, 3:4], ALU.is_lt, ALU.mult))
            link(v.tensor_tensor(part_w[:, 0:1], part_w[:, 0:1], part_w[:, 1:2], ALU.add))
            link(v.tensor_copy(wf1_h, wf1_f))
            link(v.scalar_tensor_tensor(wf1_f, wf1_h, part_w[:, 0:1], wf1_f, ALU.mult, ALU.subtract))
            link(v.tensor_copy(wf1_h, wf1_f))
            link(v.scalar_tensor_tensor(wf1_sb, wf1_h, part_w[:, 2:3], wf1_f, ALU.mult, ALU.subtract))
            deinterleave(wf2_sb, wf2_raw)
            deinterleave(bf2_f, bf2_t)
            link(v.memset(bf2_b, 0.0))
            for k in range(3):
                link(v.tensor_copy(bf2_p, bf2_f))
                if k < 2:
                    link(v.tensor_tensor(bf2_f, bf2_f, bf2_p, ALU.subtract))
                link(v.scalar_tensor_tensor(bf2_b, bf2_p, ident[0:3, k:k + 1], bf2_b, ALU.mult, ALU.add))
            v.memset(stat, 1.0).then_inc(l3w_ready, 1)
            dve.wait_ge(l3w_ready, 2)

            def hidden(i, s):
                gi = 2 * i + s
                dve.wait_ge(sp_ready, gi + 1)
                if not (isinstance(gi, int) and gi < 2):
                    dve.wait_ge(filt_done, GROUP * (gi - 1))
                v.scalar_tensor_tensor(hT[:, s, :], bank[1], 0.0, sp, ALU.max, ALU.add).then_inc(h_ready, 1)

            def one_hot(i, s, c):
                n = GROUP * (2 * i + s) + c
                if c == 0:
                    dve.wait_ge(side_ready, 2 * i + s + 1)
                if not (isinstance(n, int) and n < GROUP):
                    dve.wait_ge(scat_chunk, n - GROUP + 1)
                v.tensor_scalar(oh[:, c, :], iota[:, :], side[:, s, c, C_SRC - ATT:C_SRC - ATT + 1], side[:, s, c, C_R - ATT:C_R - ATT + 1],
                                ALU.is_equal, ALU.mult).then_inc(oh_ready, 1)

            def messages(i, s, c, nxt=None):
                n = GROUP * (2 * i + s) + c
                b = bank[2 + c]
                y = [side[:, s, c, C_Y - ATT + k:C_Y - ATT + k + 1] for k in range(3)]
                vk = [zg[:, s, c, (1 + k) * P:(2 + k) * P] for k in range(3)]
                dve.wait_ge(z_in[s][c], 16 * (i + 1))
                v.tensor_scalar(vy[:, c, :], vk[0], y[0], None, ALU.mult).then_inc(vy_chain, 1)
                dve.wait_ge(vy_chain, 3 * n + 1)
                v.scalar_tensor_tensor(vy[:, c, :], vk[1], y[1], vy[:, c, :], ALU.mult, ALU.add).then_inc(vy_chain, 1)
                dve.wait_ge(filt_done, n + 1)
                if not (isinstance(n, int) and n < GROUP):
                    dve.wait_ge(cmul_ready, n - GROUP + 1)
                both = msg[:, c, 0:MSG + P].rearrange("p (a n) -> p a n", n=P)[:, 0:9:8, :]
                v.tensor_tensor(both, zg[:, s, c, 0:P].unsqueeze(1).to_broadcast([P, 2, P]),
                                b[:, 0:2 * P].rearrange("p (a n) -> p a n", a=2), ALU.mult).then_inc(msg_a, 1)
                v.tensor_tensor(msg[:, c, 5 * P:8 * P].rearrange("p (a n) -> p a n", a=3),
                                zg[:, s, c, P:4 * P].rearrange("p (a n) -> p a n", a=3),
                                b[:, 3 * P:4 * P].unsqueeze(1).to_broadcast([P, 3, P]), ALU.mult)
                if nxt:
                    hidden(*nxt)
                dve.wait_ge(vy_chain, 3 * n + 2)
                v.scalar_tensor_tensor(vy[:, c, :], vk[2], y[2], vy[:, c, :], ALU.mult, ALU.add).then_inc(vy_chain, 1)
                dve.wait_ge(vy_chain, 3 * n + 3)
                v.tensor_tensor(msg[:, c, P:2 * P], vy[:, c, :], b[:, 2 * P:3 * P], ALU.mult).then_inc(msg_ready, 1)

            def add_sums(i, s):
                gi = 2 * i + s
                off = dve.value_load(offs[1][0:1, ds(gi, 1)], min_val=0, max_val=(NT - 1) * MSG)
                dve.wait_ge(scat_chunk, GROUP * (gi + 1))
                if isinstance(gi, int) and gi == 0:
                    dve.wait_ge(agg_zero, 1)
                else:
                    dve.wait_ge(agg_added, gi)
                a = agg[:, ds(off, MSG)]
                v.tensor_tensor(a, a, ps67[:, :], ALU.add).then_inc(agg_added, 1)

            def group(i, s, head=False, tail=False):
                one_hot(i, s, 0)
                messages(i, s, 0)
                if not head:
                    add_sums(i if s == 1 else i - 1, 1 - s)
                for c in range(1, GROUP):
                    one_hot(i, s, c)
                    messages(i, s, c, nxt=(i if s == 0 else i + 1, 1 - s) if c == GROUP - 1 and not tail else None)

            hidden(0, 0)
            group(0, 0, head=True)
            group(0, 1)
            with dve.Fori(1, L3_IT - 1) as i:
                group(i, 0)
                group(i, 1)
            group(L3_IT - 1, 0)
            group(L3_IT - 1, 1, tail=True)
            add_sums(L3_IT - 1, 1)


            def activated(t):
                s = t % 2
                dve.wait_ge(act_sv, 2 * t + 2)
                v.scalar_tensor_tensor(svT[:, s, 0:P], bank[2 + 4 * s][:, 0:P], 0.0, sp[:, s * P:(s + 1) * P], ALU.max, ALU.add).then_inc(svT_ready, 1)

            def finish(t):
                s, r = t % 2, rows_of(t)
                dve.wait_ge(o_done, t + 1)
                y, o = xa[0:r, t, :], bank[3 + 4 * s]
                link(v.tensor_tensor(y[:, 0:P], o[0:r, 0:P], y[:, 0:P], ALU.add))
                yv = y[:, P:D].rearrange("p (d i) -> p i d", i=3)
                v.tensor_tensor(yv, o[0:r, P:D].rearrange("p (i d) -> p i d", i=3), yv, ALU.add).then_inc(o_read, 1)
                dve.wait_ge(o_read, t + 1)
                link(v.bn_stats(lnt[0:r, 0:6], y))
                link(v.bn_aggr(stat[0:r, :, t], lnt[0:r, 0:6]))

            activated(0)
            for t in range(NT):
                if t + 1 < NT:
                    activated(t + 1)
                finish(t)
            v.tensor_scalar(stat[:, 1, :], stat[:, 1, :], EPS, None, ALU.add).then_inc(var_ready, 1)
            dve.wait_ge(std_ready, 3 * NT + 1)
            link(v.reciprocal(stat[:, 1, :], stat[:, 1, :]))
            for t in range(NT):
                y = xa[0:rows_of(t), t, :]
                r = rows_of(t)
                v.tensor_scalar(y, y, stat[0:r, 0, t:t + 1], stat[0:r, 1, t:t + 1], ALU.subtract, ALU.mult).then_inc(y_ready, 1)


def kernel(x, src, dst, edge_attr_20, edge_attr_3, edge_weight, L0_gnn_W1, L0_gnn_b1, L0_gnn_W2, L0_gnn_b2,
           L1_gnn_W_self1, L1_gnn_W_neigh1, L1_gnn_b1, L1_gnn_W_self2, L1_gnn_W_neigh2, L1_gnn_b2,
           L2_gnn_W, L2_gnn_bias, L3_gnn_W_in2f_s, L3_gnn_W_in2f_v, L3_gnn_Wf1, L3_gnn_bf1, L3_gnn_Wf2, L3_gnn_bf2,
           L3_gnn_W1_s, L3_gnn_W1_v, L3_gnn_W2_s, L3_gnn_W2_v):
    import concourse.bacc as _bacc
    from concourse.bass_utils import run_bass_kernel_spmd as _run

    given = dict(x=x, src=src, dst=dst, edge_attr_20=edge_attr_20, edge_attr_3=edge_attr_3, edge_weight=edge_weight,
                 l0_w1=L0_gnn_W1, l0_b1=L0_gnn_b1, l0_w2=L0_gnn_W2, l0_b2=L0_gnn_b2,
                 l1_ws1=L1_gnn_W_self1, l1_wn1=L1_gnn_W_neigh1, l1_b1=L1_gnn_b1,
                 l1_ws2=L1_gnn_W_self2, l1_wn2=L1_gnn_W_neigh2, l1_b2=L1_gnn_b2,
                 l2_w=L2_gnn_W, l2_b=L2_gnn_bias, w_in_s=L3_gnn_W_in2f_s, w_in_v=L3_gnn_W_in2f_v,
                 wf1=L3_gnn_Wf1, bf1=L3_gnn_bf1, wf2=L3_gnn_Wf2, bf2=L3_gnn_bf2,
                 w1_s=L3_gnn_W1_s, w1_v=L3_gnn_W1_v, w2_s=L3_gnn_W2_s, w2_v=L3_gnn_W2_v)
    nc = _bacc.Bacc("TRN2", target_bir_lowering=False, num_devices=1)
    arrays, aps = {}, {}
    for name, a in given.items():
        a = np.ascontiguousarray(a)
        arrays["in_" + name] = a
        aps[name] = nc.dram_tensor("in_" + name, a.shape, mybir.dt.from_np(a.dtype), kind="ExternalInput").ap()
    aps["out"] = nc.dram_tensor("out_x", (N, D), mybir.dt.float32, kind="ExternalOutput").ap()
    build(nc, **aps)
    r = _run(nc, [arrays], core_ids=[0])
    return r.results[0]["out_x"]
```
